# Optimizing a Trainium2 kernel written in Bass

```python
import numpy as np
import jax
import jax.numpy as jnp

def _softmax(x, axis=-1):
    return jax.nn.softmax(x, axis=axis)

def _gelu(x):
    return jax.nn.gelu(x, approximate=True)

def _silu(x):
    return jax.nn.silu(x)

def _sigmoid(x):
    return jax.nn.sigmoid(x)

def _layernorm(x, axis=-1, eps=1e-05):
    m = jnp.mean(x, axis=axis, keepdims=True)
    v = jnp.var(x, axis=axis, keepdims=True)
    return (x - m) / jnp.sqrt(v + eps)

def _scatter_add(tgt, idx, src, axis=0):
    return tgt.at[idx].add(src)

def _segment_sum(src, seg, n):
    return jax.ops.segment_sum(src, seg, n)
kernel_name = 'mk_adj_preln_d2_adj_r2_49671b'

def setup_inputs(seed: int=0):
    np.random.seed(seed)
    _w = jnp.asarray

    def _rec_inputs():
        import jax
        import jax.numpy as jnp
        _gk = jax.random.key(seed)
        x = 0.0002141 + 1 * jax.random.normal(jax.random.fold_in(_gk, 1), (8192, 128), jnp.float32)
        _a = jax.random.bernoulli(jax.random.fold_in(_gk, 2), 0.000976562, (8192, 8192))
        adj = _a.astype(jnp.int32)
        return (x, adj)
    x, adj = _rec_inputs()

    def _L0_gnn_setup():
        import jax, jax.numpy as jnp
        import numpy as np
        NUM_NODES = 3072
        INPUT_DIM = 128
        OUTPUT_DIM = 128
        NUM_HEADS = 4
        HEAD_DIM = OUTPUT_DIM // NUM_HEADS
        NEG_INF = -9000000000000000.0
        key = jax.random.key(seed)
        k_x, k_adj, k_W, k_a = jax.random.split(key, 4)
        x = jax.random.normal(k_x, (NUM_NODES, INPUT_DIM), dtype=jnp.float32)
        adj = jax.random.randint(k_adj, (NUM_NODES, NUM_NODES), 0, 2, dtype=jnp.int32)
        W = jax.random.uniform(k_W, (NUM_HEADS, INPUT_DIM, HEAD_DIM), dtype=jnp.float32, minval=-1.0, maxval=1.0) * np.sqrt(6.0 / INPUT_DIM)
        a = jax.random.uniform(k_a, (NUM_HEADS, 2 * HEAD_DIM, 1), dtype=jnp.float32, minval=-1.0, maxval=1.0) * np.sqrt(6.0 / (2 * HEAD_DIM))
        return {'x': x, 'adj': adj, 'W': W, 'a': a}
    _L0_gnn_all = _L0_gnn_setup()
    _L0_gnn_in = {k: v for k, v in _L0_gnn_all.items() if k in ('W', 'a')}
    del _L0_gnn_all

    def _L1_gnn_setup():
        import jax, jax.numpy as jnp
        import numpy as np
        N = 4096
        D_IN = 128
        D_HID = 128
        D_OUT = 128
        key = jax.random.key(seed)
        k_x, k_a, k0, k1, k2, k3 = jax.random.split(key, 6)
        x = jax.random.normal(k_x, (N, D_IN), dtype=jnp.float32)
        adj_matrix = jax.random.randint(k_a, (N, N), 0, 2, dtype=jnp.int32)
        s0 = 1.0 / np.sqrt(D_IN)
        s1 = 1.0 / np.sqrt(D_HID)
        w_self_0 = jax.random.uniform(k0, (D_HID, D_IN), jnp.float32, -s0, s0)
        w_neigh_0 = jax.random.uniform(k1, (D_HID, D_IN), jnp.float32, -s0, s0)
        w_self_1 = jax.random.uniform(k2, (D_OUT, D_HID), jnp.float32, -s1, s1)
        w_neigh_1 = jax.random.uniform(k3, (D_OUT, D_HID), jnp.float32, -s1, s1)
        return {'x': x, 'adj_matrix': adj_matrix, 'w_self_0': w_self_0, 'w_neigh_0': w_neigh_0, 'w_self_1': w_self_1, 'w_neigh_1': w_neigh_1}
    _L1_gnn_all = _L1_gnn_setup()
    _L1_gnn_in = {k: v for k, v in _L1_gnn_all.items() if k in ('w_self_0', 'w_neigh_0', 'w_self_1', 'w_neigh_1')}
    del _L1_gnn_all
    return {'x': x, 'adj': adj, 'L0_gnn_W': _L0_gnn_in['W'], 'L0_gnn_a': _L0_gnn_in['a'], 'L1_gnn_w_self_0': _L1_gnn_in['w_self_0'], 'L1_gnn_w_neigh_0': _L1_gnn_in['w_neigh_0'], 'L1_gnn_w_self_1': _L1_gnn_in['w_self_1'], 'L1_gnn_w_neigh_1': _L1_gnn_in['w_neigh_1']}

def reference(x, adj, L0_gnn_W, L0_gnn_a, L1_gnn_w_self_0, L1_gnn_w_neigh_0, L1_gnn_w_self_1, L1_gnn_w_neigh_1):
    import jax
    import jax.numpy as jnp

    def _L0_gnn_ref(x, adj, W, a):
        import jax, jax.numpy as jnp
        import numpy as np
        NUM_NODES = 3072
        INPUT_DIM = 128
        OUTPUT_DIM = 128
        NUM_HEADS = 4
        HEAD_DIM = OUTPUT_DIM // NUM_HEADS
        NEG_INF = -9000000000000000.0
        H, Din, d = W.shape
        N = x.shape[0]
        h = jnp.einsum('ni,hid->hnd', x, W)
        a_dst = a[:, :d, 0]
        a_src = a[:, d:, 0]
        s_dst = jnp.einsum('hnd,hd->hn', h, a_dst)
        s_src = jnp.einsum('hnd,hd->hn', h, a_src)
        energy = jax.nn.leaky_relu(s_src[:, :, None] + s_dst[:, None, :], negative_slope=0.2)
        energy = jnp.where(adj[None] > 0, energy, NEG_INF)
        attention = jax.nn.softmax(energy, axis=-1)
        h_prime = jnp.einsum('hij,hjd->hid', attention, h)
        return jnp.reshape(h_prime, (N, H * d))

    def _L1_gnn_ref(x, adj_matrix, w_self_0, w_neigh_0, w_self_1, w_neigh_1):
        import jax, jax.numpy as jnp
        import numpy as np
        N = 4096
        D_IN = 128
        D_HID = 128
        D_OUT = 128
        A = adj_matrix.astype(x.dtype)

        def layer(h, w_self, w_neigh):
            neigh = A @ h
            return jax.nn.relu(h @ w_self.T + neigh @ w_neigh.T)
        h = layer(x, w_self_0, w_neigh_0)
        return layer(h, w_self_1, w_neigh_1)
    h = jnp.maximum(_layernorm(x, axis=-1), 0.0)
    x = x + _L0_gnn_ref(h, adj, L0_gnn_W, L0_gnn_a)
    h = jnp.maximum(_layernorm(x, axis=-1), 0.0)
    x = x + _L1_gnn_ref(h, adj, L1_gnn_w_self_0, L1_gnn_w_neigh_0, L1_gnn_w_self_1, L1_gnn_w_neigh_1)
    return x

_drawn_inputs = setup_inputs


def setup_inputs(seed=0):
    import zlib

    import numpy as np

    out = dict(_drawn_inputs(seed))
    spreads = {}
    factors = {}
    for name, (base, spread) in spreads.items():
        noise = np.random.default_rng([zlib.crc32(name.encode()), seed]).standard_normal(out[name].shape)
        drawn = base * np.exp(spread * noise) if base else spread * noise
        out[name] = jnp.asarray(drawn.astype(out[name].dtype))
    for name, factor in factors.items():
        out[name] = (out[name] * factor).astype(out[name].dtype)
    return out
```

```python
from contextlib import ExitStack

import numpy as np

import concourse.bass as bass
from concourse import mybir

ALU = mybir.AluOpType
ACT = mybir.ActivationFunctionType
AX = mybir.AxisListType
F32 = mybir.dt.float32
F16 = mybir.dt.float16
BF16 = mybir.dt.bfloat16
F8 = mybir.dt.float8e5
U16 = mybir.dt.uint16
I32 = mybir.dt.int32
RMAX = bass.bass_isa.ReduceOp.max
ds = bass.ds

P = 128
N = 8192
D = 128
NB = N // P
HEADS = 4
HD = D // HEADS
HC = HD + 1
PC = HEADS * HC + 2 * HEADS
OCT = NB // 8
PLANES = 8
QU = 4
QW = N // QU // 16
ACT_HEADS = 2
EPS = 1e-5
BIG = 2.0 ** 100
TINY = 1e-30
XSCALE = 2.0 ** 15
LSCALE = 2.0 ** 11
HSCALE = 2.0 ** 12
H1MAX = 2.0 ** 15
SLOTS = 4
CHUNK = 4
GROUPS = QU * 4
HEAD_STEPS = 24
OCTETS = 32
BANKW = 462


def cast_step(o):
    return HEAD_STEPS + o * (NB - HEAD_STEPS) // OCTETS


CAST_AT = {cast_step(o): o for o in range(OCTETS)}
assert len(CAST_AT) == OCTETS
PRE_ACT_OCTETS = (1, 4, 6)
ACT_OCTETS = ()
PRE = NB // QU * 8
EP = 19


M_AT = {}
for _k in range(4):
    M_AT[_k, 0] = (_k, 264)
for _i, _kh in enumerate([(0, 1), (0, 2), (1, 1), (1, 2), (2, 1), (2, 2), (3, 1), (3, 2), (3, 3)]):
    M_AT[_kh] = (4 + _i // 3, 132 * (_i % 3))


def pieces(k):
    out = [(None, (0, 1), k, 0)]
    for h in range(HEADS):
        if (k, h) in M_AT:
            out.append((h, (0, 1), *M_AT[k, h]))
        else:
            out.append((h, (0,), k, 396))
            out.append((h, (1,), 4 + k, 396))
    return out


def input_stage(nc, mem, x, W, a, ident, srow_dram):
    X, TB, NT, AB, MEAN, HMAX = mem["X"], mem["TB"], mem["NT"], mem["AB"], mem["MEAN"], mem["HMAX"]
    with ExitStack() as ctx:
        sb = lambda n, s, d: ctx.enter_context(nc.sbuf_tensor(n, s, d))
        ps = lambda n, s: ctx.enter_context(nc.psum_tensor(n, s, F32))
        sem = lambda n: ctx.enter_context(nc.semaphore(n))
        space = mem["PK"][:].rearrange("p u q w -> p (u q w)").bitcast(F32)
        XQ = space[:, 0:NB * D].rearrange("p (q d) -> p q d", d=D)
        HF = sb("HF", [P, NB, PC], F32)
        MV = sb("MV", [P, NB, 2], F32)
        ST = sb("ST", [P, 2, 6], F32)
        RS = sb("RS", [P, NB], F32)
        NM = sb("NM", [P, NB], F32)
        HB = sb("HB", [P, 2, 4, D], F32)
        HT = sb("HT", [P, 2, 512], F32)
        SR = sb("SR", [HEADS, 2, 512], F32)
        WC = sb("WC", [P, PC], F32)
        WF = sb("WF", [P, HEADS, HD], F32)
        WT = sb("WT", [P, P], F32)
        ABL = sb("ABL", [P, 2 * HEADS], F32)
        ID = sb("ID", [P, P], F32)
        ONES = sb("ONES", [P, P], F32)
        EPSC = sb("EPSC", [P, 1], F32)
        MX = sb("MX", [P, 6], F32)
        GM = sb("GM", [P, 6], F32)
        NEGT = sb("NEGT", [P, 8], F32)
        EB = sb("EB", [P, 2, NB, HEADS], F32)
        Y = sb("Y", [P, 2, NB, HEADS], F32)
        YS = sb("YS", [P, NB, HEADS], F32)
        RH = sb("RH", [P, 1], F32)
        FULL = space[:, NB * D:NB * D + 2 * NB * HC].rearrange("p (i q c) -> p i q c", i=2, c=HC)
        PT = ps("PT", [P, 2, 512])
        PP = ps("PP", [P, 4, 512])
        PR = ps("PR", [P, 2, 512])

        x_in, w_in, w_mem, v_ps, v_sb = sem("x_in"), sem("w_in"), sem("w_mem"), sem("v_ps"), sem("v_sb")
        stats, moments, std, norm_ready = sem("stats"), sem("moments"), sem("std"), sem("norm_ready")
        h_ready, turned, ht_ready, projected = sem("h_ready"), sem("turned"), sem("ht_ready"), sem("projected")
        hf_ready, srows_ps, sr_ready = sem("hf_ready"), sem("srows_ps"), sem("sr_ready")
        sr_out = [sem("sr_out0"), sem("sr_out1")]
        maxima, all_max, neg_max, scales = sem("maxima"), sem("all_max"), sem("neg_max"), sem("scales")
        row_args, exps, full, hi_done = sem("row_args"), sem("exps"), sem("full"), sem("hi_done")
        lo_done, mean_ps = sem("lo_done"), sem("mean_ps")
        def hf_credit(i, s):
            return i * 4 + 2 * s + 1

        x_q = x.rearrange("(u t b e) d -> b u t e d", u=OCT, t=8, b=PLANES, e=16)
        block = ctx.enter_context(nc.Block())

        @block.sync
        def _(sp):
            for q in sr_out:
                sp.sem_inc(q, 16)
            sp.dma_start(ID[:], ident).then_inc(w_in, 16)
            sp.dma_start(WF[:], W.rearrange("h i d -> i h d")).then_inc(w_in, 16)
            sp.wait_ge(w_mem, 2)
            for s in range(2):
                for h in range(HEADS):
                    sp.dma_start(ABL[HD * h:HD * h + HD, HEADS * s + h:HEADS * s + h + 1],
                                 a[h, HD * s:HD * s + HD, :]).then_inc(w_in, 16)
            with nc.sync.Fori(0, PLANES) as b:
                for u in range(OCT):
                    sp.dma_start(XQ[:, ds(b * OCT + u, 1), :].squeeze(1), x_q[b, u]).then_inc(x_in, 16)
            with nc.sync.Fori(0, 8) as i:
                for s in range(2):
                    sp.wait_ge(sr_ready, i * 2 + s + 1)
                    sp.dma_start(srow_dram[:, ds(i * 1024 + s * 512, 512)], SR[:, s, :]).then_inc(sr_out[s], 16)
            sp.wait_ge(sr_out[0], 128 + 16)
            sp.wait_ge(sr_out[1], 128 + 16)

        @block.tensor
        def _(pe):
            pe.wait_ge(w_in, 160)
            pe.transpose(PT[:, 0, 0:P], WF[:].rearrange("p h d -> p (h d)"), ID[:]).then_inc(v_ps, 1)
            pe.wait_ge(v_sb, 1)
            pe.matmul(PT[:, 1, 0:2 * HEADS], WT[:], ABL[:], start=True, stop=True).then_inc(v_ps, 1)
            pe.wait_ge(v_sb, 3)
            with nc.tensor.Fori(0, 8) as i:
                for s in range(2):
                    pe.wait_ge(h_ready, i * 2 + s + 1)
                    for k in range(4):
                        mm = pe.transpose(PT[:, s, k * P:(k + 1) * P], HB[:, s, k, :], ID[:])
                    mm.then_inc(turned, 1)
                    pe.wait_ge(ht_ready, i * 2 + s + 1)
                    pe.wait_ge(hf_ready, hf_credit(i, s))
                    for k in range(4):
                        mm = pe.matmul(PP[:, 2 * s + k // 2, (k % 2) * PC:(k % 2) * PC + PC],
                                       HT[:, s, k * P:(k + 1) * P], WC[:], start=True, stop=True)
                    mm.then_inc(projected, 1)
                    pe.matmul(PR[0:HEADS, s, :], WC[:, PC - HEADS:PC], HT[:, s, :],
                              start=True, stop=True).then_inc(srows_ps, 1)
            pe.wait_ge(hf_ready, 2 * 16 + 3)
            for qb in range(NB):
                mm = pe.matmul(PT[:, 0, 0:HEADS * HC], ONES[:], HF[:, qb, 0:HEADS * HC],
                               start=(qb == 0), stop=(qb == NB - 1))
            mm.then_inc(mean_ps, 1)

        @block.scalar
        def _(act):
            act.wait_ge(moments, NB)
            act.wait_ge(w_mem, 4)
            act.activation(RS[:], MV[:, :, 1], ACT.Sqrt, bias=EPSC[:]).then_inc(std, 1)
            act.wait_ge(norm_ready, 2)
            with nc.scalar.Fori(0, 8) as i:
                for s in range(2):
                    act.wait_ge(hf_ready, hf_credit(i, s))
                    for k in range(4):
                        qb = i * 8 + 4 * s + k
                        a_ = act.activation(HB[:, s, k, :], XQ[:, ds(qb, 1), :].squeeze(1), ACT.Relu,
                                            bias=NM[:, ds(qb, 1)], scale=RS[:, ds(qb, 1)])
                    a_.then_inc(h_ready, 1)
                    act.wait_ge(srows_ps, i * 2 + s + 1)
                    act.wait_ge(sr_out[s], i * 16 + 16)
                    act.copy(SR[:, s, :], PR[0:HEADS, s, :]).then_inc(sr_ready, 1)
            act.wait_ge(neg_max, 2)
            for h in range(HEADS):
                t_h = HF[:, :, HEADS * HC + h]
                act.activation(EB[:, 0, :, h], t_h, ACT.Exp, bias=NEGT[:, h:h + 1]).then_inc(exps, 1)
                act.activation(EB[:, 1, :, h], t_h, ACT.Exp, bias=NEGT[:, 4 + h:5 + h], scale=0.2).then_inc(exps, 1)
            act.wait_ge(row_args, 2)
            for c in range(2):
                act.activation(AB[:].rearrange("p q (h c) -> p q h c", c=2)[:, :, :, c], Y[:, c], ACT.Exp) \
                   .then_inc(exps, 1)
            for j in range(2 * HEADS):
                h, c = j // 2, j % 2
                act.wait_ge(full, j + 1)
                act.activation(X[:, :, 0, h, c * HC:(c + 1) * HC], FULL[:, j % 2], ACT.Copy,
                               scale=1.0 / LSCALE).then_inc(hi_done, 1)

        @block.gpsimd
        def _(pool):
            pool.memset(WC[:], 0.0).then_inc(w_mem, 1)
            pool.memset(ABL[:], 0.0).then_inc(w_mem, 1)
            pool.memset(ONES[:], 1.0).then_inc(w_mem, 1)
            pool.memset(EPSC[:], EPS).then_inc(w_mem, 1)
            pool.wait_ge(maxima, 3)
            pool.partition_all_reduce(GM[:], MX[:], P, RMAX).then_inc(all_max, 1)

        @block.vector
        def _(dve):
            dve.sem_inc(hf_ready, 3)
            dve.wait_ge(w_mem, 1)
            dve.wait_ge(v_ps, 1)
            dve.tensor_copy(WT[:], PT[:, 0, 0:P]).then_inc(v_sb, 1)
            dve.tensor_copy(WC[:, 0:HEADS * HC].rearrange("p (h c) -> p h c", c=HC)[:, :, 0:HD], WF[:]) \
               .then_inc(v_sb, 1)
            dve.wait_ge(v_ps, 2)
            dve.tensor_copy(WC[:, HEADS * HC:PC], PT[:, 1, 0:2 * HEADS]).then_inc(v_sb, 1)
            dve.wait_ge(x_in, 16 * NB)
            for qb in range(NB):
                if qb >= 2:
                    dve.wait_ge(moments, qb - 1)
                dve.bn_stats(ST[:, qb % 2, :], XQ[:, qb, :]).then_inc(stats, 1)
                if qb >= 1:
                    dve.wait_ge(stats, qb)
                    dve.bn_aggr(MV[:, qb - 1, :], ST[:, (qb - 1) % 2, :]).then_inc(moments, 1)
            dve.wait_ge(stats, NB)
            dve.bn_aggr(MV[:, NB - 1, :], ST[:, (NB - 1) % 2, :]).then_inc(moments, 1)
            dve.wait_ge(std, 1)
            dve.reciprocal(RS[:], RS[:]).then_inc(norm_ready, 1)
            dve.wait_ge(norm_ready, 1)
            dve.scalar_tensor_tensor(NM[:], MV[:, :, 0], -1.0, RS[:], ALU.mult, ALU.mult).then_inc(norm_ready, 1)
            with nc.vector.Fori(0, 8) as i:
                for s in range(2):
                    dve.wait_ge(turned, i * 2 + s + 1)
                    dve.tensor_copy(HT[:, s, :], PT[:, s, :]).then_inc(ht_ready, 1)
                    dve.wait_ge(projected, i * 2 + s + 1)
                    for k in range(2):
                        dve.tensor_copy(HF[:, ds(i * 8 + 4 * s + 2 * k, 2), :],
                                        PP[:, 2 * s + k, 0:2 * PC].rearrange("p (k c) -> p k c", c=PC)) \
                           .then_inc(hf_ready, 1)
            dve.wait_ge(hf_ready, 2 * 16 + 3)
            tcol = HF[:, :, HEADS * HC:HEADS * HC + HEADS]
            scol = HF[:, :, PC - HEADS:PC]
            feats = HF[:, :, 0:HEADS * HC]
            dve.tensor_reduce(MX[:, 0:4], tcol.rearrange("p q h -> p h q"), AX.X, ALU.max).then_inc(maxima, 1)
            dve.tensor_reduce(MX[:, 4:5], feats, AX.XY, ALU.max).then_inc(maxima, 1)
            dve.tensor_reduce(MX[:, 5:6], feats, AX.XY, ALU.min, negate=True).then_inc(maxima, 1)
            dve.wait_ge(all_max, 1)
            dve.tensor_scalar(NEGT[:, 0:4], GM[:, 0:4], -1.0, None, ALU.mult).then_inc(neg_max, 1)
            dve.tensor_scalar(NEGT[:, 4:8], GM[:, 0:4], -0.2, None, ALU.mult).then_inc(neg_max, 1)
            dve.tensor_scalar(HMAX[:], GM[:, 4:5], GM[:, 5:6], TINY, ALU.max, ALU.max).then_inc(scales, 1)
            dve.tensor_tensor(YS[:], scol, GM[:, 0:4].unsqueeze(1).broadcast_to([P, NB, HEADS]), ALU.add) \
               .then_inc(scales, 1)
            dve.wait_ge(scales, 1)
            dve.reciprocal(RH[:], HMAX[:]).then_inc(scales, 1)
            dve.wait_ge(scales, 2)
            dve.tensor_scalar(Y[:, 0], YS[:], 0.8, 0.0, ALU.mult, ALU.min).then_inc(row_args, 1)
            dve.tensor_scalar(Y[:, 1], YS[:], -0.8, 0.0, ALU.mult, ALU.min).then_inc(row_args, 1)
            dve.tensor_scalar(TB[:], tcol, BIG, None, ALU.mult).then_inc(scales, 1)
            dve.tensor_scalar(NT[:], tcol, -1.0, None, ALU.mult).then_inc(scales, 1)
            dve.wait_ge(exps, 8)
            dve.wait_ge(scales, 3)
            dve.tensor_scalar(EB[:], EB[:], RH[:], XSCALE * LSCALE, ALU.mult, ALU.mult).then_inc(scales, 1)
            dve.wait_ge(mean_ps, 1)
            dve.tensor_scalar(MEAN[:].rearrange("p (h c) -> p h c", c=HD),
                              PT[:, 0, 0:HEADS * HC].rearrange("p (h c) -> p h c", c=HC)[:, :, 0:HD],
                              1.0 / N, None, ALU.mult).then_inc(scales, 1)
            dve.tensor_copy(feats.rearrange("p q (h c) -> p q h c", c=HC)[:, :, :, HD],
                            HMAX[:].unsqueeze(2).broadcast_to([P, NB, HEADS])).then_inc(scales, 1)
            dve.wait_ge(scales, 8)
            for j in range(2 * HEADS + 1):
                if j < 2 * HEADS:
                    h, c = j // 2, j % 2
                    if j >= 2:
                        dve.wait_ge(lo_done, j - 1)
                    dve.tensor_tensor(FULL[:, j % 2], HF[:, :, h * HC:(h + 1) * HC],
                                      EB[:, c, :, h].unsqueeze(2).broadcast_to([P, NB, HC]), ALU.mult) \
                       .then_inc(full, 1)
                if j >= 1:
                    h, c = (j - 1) // 2, (j - 1) % 2
                    dve.wait_ge(hi_done, j)
                    dve.scalar_tensor_tensor(X[:, :, 1, h, c * HC:(c + 1) * HC],
                                             X[:, :, 0, h, c * HC:(c + 1) * HC],
                                             -LSCALE, FULL[:, (j - 1) % 2], ALU.mult, ALU.add).then_inc(lo_done, 1)


def heads_q(v):
    v = v.rearrange("(h m) (c d) -> h (m c) d", h=HEADS, c=HEADS)
    return v.rearrange("h (u t b e) d -> b u h t e d", u=OCT, t=8, b=PLANES, e=16)


def attention_stage(nc, mem, x, adj, packw, srow_dram, x1_dram):
    X, TB, NT, AB, MEAN, HMAX, PK = (mem[n] for n in ("X", "TB", "NT", "AB", "MEAN", "HMAX", "PK"))
    with ExitStack() as ctx:
        sb = lambda n, s, d: ctx.enter_context(nc.sbuf_tensor(n, s, d))
        sem = lambda n: ctx.enter_context(nc.semaphore(n))
        AI = sb("AI", [P, 2, 2, 1024], I32)
        CA = sb("CA", [P, 4, 8, P], F8)
        PW = sb("PW", [P, 8], BF16)
        AU = sb("AU", [P, 2, CHUNK, 2, QW], U16)
        MK = sb("MK", [P, SLOTS, HEADS, 512], F8)
        SN = sb("SN", [P, HEADS, 2, 256], F32)
        SA = sb("SA", [P, ACT_HEADS, 512], F32)
        SD = sb("SD", [P, HEADS - ACT_HEADS, 512], F32)
        EV = sb("EV", [P, 7, BANKW], F32)
        MC = sb("MC", [P, 16, 2, HC], F32)
        AC = sb("AC", [P, 16, HC], F32)
        XG = sb("XG", [P, 4, D], F32)
        TM = sb("TM", [P, 16, HD], F32)
        SM = sb("SM", [P, 2, 16], F32)
        acc = [ctx.enter_context(nc.psum_tensor(f"acc{i}", [P, 512], F32)) for i in range(7)]
        PKP = ctx.enter_context(nc.psum_tensor("PKP", [P, NB, 8], F32))

        consts_in = sem("consts_in")
        waited = sem("waited")
        adj_in = [sem("adj_in0"), sem("adj_in1")]
        cast_ready = [sem(f"cast_ready{i}") for i in range(4)]
        cast_free = sem("cast_free")
        pk_ready = sem("pk_ready")
        s_in, sa_ready, sd_ready = sem("s_in"), sem("sa_ready"), sem("sd_ready")
        unpacked, unpacked_free = sem("unpacked"), sem("unpacked_free")
        gt_act, gt_dve = sem("gt_act"), sem("gt_dve")
        masks_ready, masks_free = sem("masks_ready"), sem("masks_free")
        acc_done = sem("acc_done")
        ev_dve, ev_act = sem("ev_dve"), sem("ev_act")
        ep = sem("ep")
        xg_in, x1_out = sem("xg_in"), sem("x1_out")
        block = ctx.enter_context(nc.Block())

        adj_t = adj.rearrange("(t p) (c w) -> t c p w", p=P, w=2048)
        x_q, x1_q = heads_q(x), heads_q(x1_dram)
        @block.sync
        def _(sp):
            def load_s(u, kp):
                for r in range(2):
                    for h in range(HEADS):
                        row = srow_dram[h:h + 1, ds((kp * 2 + r) * OCT * P + u * 256, 256)]
                        sp.dma_start(SN[:, h, r, :], row.broadcast_to([P, 256])).then_inc(s_in, 16)

            def load_next_s(g):
                sp.wait_ge(sa_ready, g + 1)
                sp.wait_ge(sd_ready, g + 1)
                load_s((g + 1) // 4, (g + 1) % 4)

            def load_x(g):
                for k in range(4):
                    for h in range(HEADS):
                        sp.dma_start(XG[:, k, HD * h:HD * h + HD], x_q[g % 4 * 2 + k // 2, g // 4 * 2 + k % 2, h]) \
                          .then_inc(xg_in, 16)

            def store_x1(g):
                sp.wait_ge(ep, g * EP + EP + 1)
                for k in range(4):
                    for h in range(HEADS):
                        sp.dma_start(x1_q[g % 4 * 2 + k // 2, g // 4 * 2 + k % 2, h], XG[:, k, HD * h:HD * h + HD]) \
                          .then_inc(x1_out, 16)

            def swap_x(g):
                store_x1(g)
                sp.wait_ge(x1_out, g * 256 + 256)
                load_x(g + 1)

            def load_chunk(C, t, c):
                for i in range(2):
                    sp.wait_ge(cast_ready[2 * (c % 2) + i], C + 1)
                sp.dma_start(AI[:, c % 2].rearrange("p a w -> p (a w)"), adj_t[t, c]).then_inc(adj_in[c % 2], 16)

            def load_tile(t, chunks=range(4)):
                for c in chunks:
                    load_chunk(t * 2 + c // 2, t, c)

            for q in cast_ready:
                sp.sem_inc(q, 1)
            sp.dma_start(PW[:], packw).then_inc(consts_in, 16)
            load_s(0, 0)
            load_x(0)
            with nc.sync.Fori(0, 16) as t:
                load_tile(t)
            load_next_s(0)
            for m in range(4):
                load_tile(16 + m)
            with nc.sync.Fori(1, 12) as g:
                load_next_s(g)
                load_tile(g * 4 + 16, range(2))
                swap_x(g - 1)
                load_tile(g * 4 + 16, range(2, 4))
                for m in range(1, 4):
                    load_tile(g * 4 + 16 + m)
            for g in range(12, 15):
                load_next_s(g)
                swap_x(g - 1)
            swap_x(14)
            store_x1(15)
            sp.wait_ge(x1_out, 256 * GROUPS)

        def cast_operands(o):
            src = AI[:, o // 2 % 2, o % 2].rearrange("p (t b e) -> p t b e", t=8, b=PLANES)
            return CA[:, o % 4].rearrange("p b (t e) -> p t b e", t=8), src

        def wait_cast(eng, B4, o):
            eng.wait_ge(cast_free, B4 * 4 + (o + 1))
            eng.wait_ge(adj_in[o // 2 % 2], B4 * 16 + 16 * (o // 4 + 1))
            eng.sem_inc(waited, 1)

        @block.tensor
        def _(pe):
            def pack(O4, o):
                pe.wait_ge(cast_ready[o % 4], O4 + (o // 4 + 2))
                if o % 8 == 0:
                    pe.wait_ge(pk_ready, O4 // 2 + (o // 8 + 1))
                pe.sem_inc(waited, 1)
                for b in range(8):
                    mm = pe.matmul(PKP[:, b * OCT + o % 8, :], CA[:, o % 4, b, :], PW[:], start=True, stop=True)
                mm.then_inc(cast_free, 1)

            def group(g, packs):
                for n in range(NB):
                    if packs and n - 1 in CAST_AT:
                        pack(g * 8 + PRE // 4, CAST_AT[n - 1])
                    pe.wait_ge(masks_ready, g * NB + (n + 1))
                    pe.sem_inc(waited, 1)
                    touched = set()
                    for k in range(4):
                        for h, parts, bank, col in pieces(k):
                            if n == 0 and bank not in touched:
                                if bank < 4:
                                    pe.wait_ge(ev_dve, g * 4 + (bank + 1))
                                else:
                                    pe.wait_ge(ev_act, g * 3 + (bank - 3))
                                pe.sem_inc(waited, 1)
                            lo, hi = parts[0], parts[-1] + 1
                            if h is None:
                                lhs = AU[:, n // CHUNK % 2, n % CHUNK, k // 2, :].bitcast(F8)[:, k % 2 * P:k % 2 * P + P]
                                rhs = X[:, n, :, :, HC:2 * HC]
                            else:
                                lhs = MK[:, n % SLOTS, h, k * P:(k + 1) * P]
                                rhs = X[:, n, lo:hi, h, :]
                            width = 66 * (hi - lo) * (HEADS // 2 if h is None else 1)
                            mm = pe.matmul(acc[bank][:, col:col + width], lhs, rhs,
                                           start=(n == 0 and bank not in touched), stop=(n == NB - 1),
                                           skip_group_check=True)
                            touched.add(bank)
                        if n == NB - 1 and k < 3:
                            mm.then_inc(acc_done, 1)
                    mm.then_inc(masks_free, 1)

            pe.sem_inc(cast_free, 4)
            pe.sem_inc(masks_free, SLOTS)
            pe.wait_ge(consts_in, 16)
            with nc.tensor.Fori(0, 16) as t:
                for o in range(8):
                    pack(t * 2, o)
            with nc.tensor.Fori(0, 12) as g:
                group(g, True)
            with nc.tensor.Fori(12, GROUPS) as g:
                group(g, False)

        @block.scalar
        def _(act):
            def copy_s(g):
                act.wait_ge(s_in, g * 128 + 128)
                act.copy(SA[:], SN[:, 0:ACT_HEADS].rearrange("p h r c -> p h (r c)")).then_inc(sa_ready, 1)

            def compare(g, n):
                if n == 0:
                    act.wait_ge(sa_ready, g + 1)
                act.wait_ge(masks_free, g * NB + (n + 1))
                act.sem_inc(waited, 1)
                for h in range(ACT_HEADS):
                    c = act.activation(MK[:, n % SLOTS, h, :], SA[:, h, :], ACT.Relu, bias=TB[:, n, h:h + 1],
                                       scale=BIG, saturate=False)
                c.then_inc(gt_act, 1)

            def cast(B4, o):
                wait_cast(act, B4, o)
                dst, src = cast_operands(o)
                act.activation(dst, src, ACT.Copy, saturate=False).then_inc(cast_ready[o % 4], 1)

            def keep_tile(T, u, c8):
                act.wait_ge(cast_free, T * 8 + 12)
                act.copy(PK[:, ds(u, 1), :, ds(c8, 8)].squeeze(1), PKP[:]).then_inc(pk_ready, 1)

            def start(g):
                act.wait_ge(gt_act, g * NB)
                copy_s(g)
                compare(g, 0)
                compare(g, 1)

            def steps(g, u, kp, packs):
                for n in range(2, NB):
                    compare(g, n)
                    if packs:
                        if n in CAST_AT and CAST_AT[n] % 8 in ACT_OCTETS:
                            cast(g * 8 + PRE // 4, CAST_AT[n])
                        if n - 2 in CAST_AT and CAST_AT[n - 2] % 8 == 7:
                            m = CAST_AT[n - 2] // 8
                            keep_tile(g * 4 + (16 + m), u + 1, kp * 32 + m * 8)
                if packs:
                    keep_tile(g * 4 + 19, u + 1, kp * 32 + 24)

            def copy_acc(g):
                act.wait_ge(ep, g * EP + 1)
                for bank, done in ((4, 2), (5, 3)):
                    act.wait_ge(acc_done, g * 3 + done)
                    act.copy(EV[:, bank, :], acc[bank][:, 0:BANKW]).then_inc(ev_act, 1)
                act.wait_ge(masks_free, g * NB + (NB + SLOTS))
                act.copy(EV[:, 6, :], acc[6][:, 0:BANKW]).then_inc(ev_act, 1)

            act.sem_inc(pk_ready, 1)
            act.sem_inc(ev_act, 3)
            with nc.scalar.Fori(0, 16) as t:
                for o in PRE_ACT_OCTETS:
                    cast(t * 2, o)
                keep_tile(t, 0, t * 8)
            copy_s(0)
            compare(0, 0)
            compare(0, 1)
            with nc.scalar.Fori(0, 3) as u:
                with nc.scalar.Fori(0, 4) as kp:
                    g = u * 4 + kp
                    steps(g, u, kp, True)
                    start(g + 1)
                    copy_acc(g)
            with nc.scalar.Fori(12, 15) as g:
                steps(g, 0, 0, False)
                start(g + 1)
                copy_acc(g)
            steps(15, 0, 0, False)
            copy_acc(15)

        @block.vector
        def _(dve):
            AB4 = AB[:].rearrange("p (b u) c -> p b u c", u=OCT)

            def unpack(u, kp, q, r):
                Q = u * 64 + (kp * 16 + q)
                b = 2 * kp + r
                dve.wait_ge(masks_free, Q * CHUNK)
                dve.tensor_scalar(AU[:, q % 2, :, r, :], PK[:, ds(u, 1), CHUNK * q:CHUNK * q + CHUNK, :].squeeze(1),
                                  abs(6 - b), 0x4040,
                                  ALU.logical_shift_left if b <= 6 else ALU.logical_shift_right,
                                  ALU.bitwise_and).then_inc(unpacked, 1)

            def compare(u, kp, n):
                S = u * 256 + (kp * NB + n)
                if n == 0:
                    dve.wait_ge(sd_ready, u * 4 + (kp + 1))
                dve.wait_ge(masks_free, S + 1)
                dve.sem_inc(waited, 1)
                for h in range(ACT_HEADS, HEADS):
                    c = dve.tensor_scalar(MK[:, n % SLOTS, h, :], SD[:, h - ACT_HEADS, :], NT[:, n, h:h + 1], 2.0,
                                          ALU.is_gt, ALU.mult, saturate=False)
                c.then_inc(gt_dve, 1)

            def mask(u, kp, n):
                S = u * 256 + (kp * NB + n)
                if n % CHUNK == 0:
                    dve.wait_ge(unpacked, u * 128 + (kp * 32 + n // CHUNK * 2 + 2))
                dve.wait_ge(gt_dve, S + 1)
                dve.wait_ge(gt_act, S + 1)
                m = MK[:, n % SLOTS].bitcast(U16)
                edges = AU[:, n // CHUNK % 2, n % CHUNK].rearrange("p r w -> p (r w)")
                dve.tensor_tensor(m, m, edges.unsqueeze(1).broadcast_to([P, HEADS, 2 * QW]), ALU.bitwise_and) \
                   .then_inc(masks_ready, 1)

            def cast(B4, o):
                wait_cast(dve, B4, o)
                dst, src = cast_operands(o)
                dve.tensor_copy(dst, src, saturate=False).then_inc(cast_ready[o % 4], 1)

            def start(u, kp):
                g = u * 4 + kp
                dve.wait_ge(s_in, g * 128 + 128)
                dve.tensor_copy(SD[:], SN[:, ACT_HEADS:].rearrange("p h r c -> p h (r c)")).then_inc(sd_ready, 1)
                if kp == 0:
                    dve.wait_ge(pk_ready, u * 16 + 17)
                for r in range(2):
                    unpack(u, kp, 0, r)
                compare(u, kp, 0)
                mask(u, kp, 0)

            def copy_acc(u, kp):
                g = u * 4 + kp
                for k in range(3):
                    dve.wait_ge(acc_done, g * 3 + (k + 1))
                    dve.tensor_copy(EV[:, k, :], acc[k][:, 0:BANKW]).then_inc(ev_dve, 1)
                dve.wait_ge(masks_free, g * NB + (NB + SLOTS))
                dve.tensor_copy(EV[:, 3, 0:396], acc[3][:, 0:396]).then_inc(ev_dve, 1)

            def epilogue(u, kp, i):
                g = u * 4 + kp
                dve.wait_ge(ep, g * EP + (i + 1))
                hi_lo = lambda out, hi, lo: dve.scalar_tensor_tensor(out, lo, 1.0 / LSCALE, hi, ALU.mult, ALU.add)
                pair = lambda bank, s0, s1: EV[:, bank, s0 * 132:s1 * 132].rearrange("p (s c x) -> p s c x", c=2, x=66)
                MCf = MC[:].rearrange("p m c x -> p m (c x)")
                if i == 0:
                    dve.wait_ge(ev_act, g * 3 + 6)
                    dve.wait_ge(ev_dve, g * 4 + 8)
                    op = hi_lo(AC[:].rearrange("p (k h) x -> p k (h x)", k=4), EV[:, 0:4, 0:132], EV[:, 0:4, 132:264])
                elif i == 1:
                    op = hi_lo(MCf.rearrange("p (k h) x -> p k h x", k=4)[:, :, 0, :], EV[:, 0:4, 264:330], EV[:, 0:4, 330:396])
                elif i == 2:
                    op = hi_lo(MCf.rearrange("p (k h) x -> p k h x", k=4)[:, 0:3, 3, :], EV[:, 0:3, 396:462], EV[:, 4:7, 396:462])
                elif i <= 7:
                    bank, s0, s1, m = [(4, 0, 2, 1), (4, 2, 3, 5), (5, 0, 1, 6), (5, 1, 3, 9), (6, 0, 3, 13)][i - 3]
                    op = hi_lo(MCf[:, m:m + s1 - s0, :], pair(bank, s0, s1)[:, :, 0, :], pair(bank, s0, s1)[:, :, 1, :])
                elif i == 8:
                    op = dve.tensor_tensor(MC[:, :, 1, :], AC[:], MC[:, :, 1, :], ALU.subtract)
                elif i == 9:
                    ab = AB4[:, 2 * kp:2 * kp + 2, ds(u * 2, 2), :].rearrange("p r u c -> p r (u c)")
                    m = MC[:].rearrange("p (r m) c x -> p r (m c) x", r=2)
                    op = dve.tensor_tensor(m, m, ab.unsqueeze(3).broadcast_to([P, 2, 16, HC]), ALU.mult)
                elif i == 10:
                    op = dve.tensor_tensor(AC[:], MC[:, :, 0, :], MC[:, :, 1, :], ALU.add)
                elif i == 11:
                    op = dve.tensor_scalar(SM[:, 0, :], AC[:, :, HD], 0.0, None, ALU.is_equal)
                elif i == 12:
                    op = dve.tensor_tensor(SM[:, 1, :], AC[:, :, HD], SM[:, 0, :], ALU.add)
                elif i == 13:
                    op = dve.reciprocal(SM[:, 1, :], SM[:, 1, :])
                elif i == 14:
                    op = dve.tensor_scalar(SM[:, 1, :], SM[:, 1, :], HMAX[:], None, ALU.mult)
                elif i == 15:
                    op = dve.tensor_tensor(TM[:], AC[:, :, 0:HD], SM[:, 1, :].unsqueeze(2).broadcast_to([P, 16, HD]), ALU.mult)
                elif i == 16:
                    dve.wait_ge(xg_in, g * 256 + 256)
                    op = dve.tensor_tensor(XG[:], XG[:], TM[:].rearrange("p (k h) x -> p k (h x)", k=4), ALU.add)
                elif i == 17:
                    mean = MEAN[:].unsqueeze(1).broadcast_to([P, 4, D]).rearrange("p k (h x) -> p k h x", h=HEADS)
                    empty = SM[:, 0, :].unsqueeze(2).broadcast_to([P, 16, HD]).rearrange("p (k h) x -> p k h x", k=4)
                    op = dve.tensor_tensor(TM[:].rearrange("p (k h) x -> p k h x", k=4), mean, empty, ALU.mult)
                elif i == 18:
                    op = dve.tensor_tensor(XG[:], XG[:], TM[:].rearrange("p (k h) x -> p k (h x)", k=4), ALU.add)
                op.then_inc(ep, 1)

            def step(u, kp, n):
                if n > 0:
                    mask(u, kp, n)
                if n < NB - 1:
                    compare(u, kp, n + 1)
                if n % CHUNK in (1, 2) and n // CHUNK + 1 < NB // CHUNK:
                    unpack(u, kp, n // CHUNK + 1, n % CHUNK - 1)

            def late_steps(u, kp, packs):
                for n in range(HEAD_STEPS, NB):
                    step(u, kp, n)
                    if packs and n in CAST_AT and CAST_AT[n] % 8 not in ACT_OCTETS:
                        cast(u * 32 + (PRE // 4 + kp * 8), CAST_AT[n])

            dve.sem_inc(ev_dve, 4)
            dve.sem_inc(ep, 1)
            with nc.vector.Fori(0, 16) as t:
                for o in range(8):
                    if o not in PRE_ACT_OCTETS:
                        cast(t * 2, o)
            dve.wait_ge(s_in, 128)
            dve.tensor_copy(SD[:], SN[:, ACT_HEADS:].rearrange("p h r c -> p h (r c)")).then_inc(sd_ready, 1)
            dve.wait_ge(pk_ready, 17)
            for r in range(2):
                dve.tensor_scalar(AU[:, 0, :, r, :], PK[:, 0, 0:CHUNK, :], 6 - r, 0x4040,
                                  ALU.logical_shift_left, ALU.bitwise_and).then_inc(unpacked, 1)
            compare(0, 0, 0)
            mask(0, 0, 0)
            for n in range(HEAD_STEPS):
                step(0, 0, n)
            with nc.vector.Fori(0, 3) as u:
                for kp in range(4):
                    late_steps(u, kp, True)
                    nu, nkp = (u, kp + 1) if kp < 3 else (u + 1, 0)
                    start(nu, nkp)
                    copy_acc(u, kp)
                    for n in range(HEAD_STEPS):
                        step(nu, nkp, n)
                        if n < EP:
                            epilogue(u, kp, n)
            for kp in range(4):
                late_steps(3, kp, False)
                if kp < 3:
                    start(3, kp + 1)
                copy_acc(3, kp)
                for n in range(HEAD_STEPS):
                    if kp < 3:
                        step(3, kp + 1, n)
                    if n < EP:
                        epilogue(3, kp, n)


def graph_stage(nc, mem, ident, ws, wn, ws1, wn1, x1_dram, out):
    PK = mem["PK"]
    with ExitStack() as ctx:
        sb = lambda n, s, d: ctx.enter_context(nc.sbuf_tensor(n, s, d))
        sem = lambda n: ctx.enter_context(nc.semaphore(n))
        HS = sb("HS", [P, NB, 2, D], F16)
        H0T = sb("H0T", [P, N], F32)
        H1T = sb("H1T", [P, N], F32)
        X1 = H1T[:].rearrange("p (q d) -> p q d", d=D)
        ED = sb("ED", [P, SLOTS, 4, 512], U16)
        WR = sb("WR", [P, 4, P], F32)
        WT = sb("WTT", [P, 4, P], F32)
        ID = sb("ID2", [P, P], F32)
        MV = sb("MV2", [P, NB, 2], F32)
        ST = sb("ST2", [P, 2, 6], F32)
        RS = sb("RS2", [P, NB], F32)
        NM = sb("NM2", [P, NB], F32)
        EPSC = sb("EPSC2", [P, 1], F32)
        ZB = sb("ZB", [P, 2, 512], F32)
        HB = sb("HB2", [P, 2, 512], F32)
        NH = sb("NH", [P, 2, 512], F32)
        OT = sb("OT", [P, 2, 512], F32)
        XL = sb("XL", [P, 4, 4, D], F32)
        CM = sb("CM", [P, 16], F32)
        SC = sb("SC", [P, 3], F32)
        bank = [ctx.enter_context(nc.psum_tensor(f"bank{i}", [P, 512], F32)) for i in range(8)]

        waited = sem("waited2")
        consts_in, x1_in, eps_set, w_turned, w_ready = (
            sem("consts_in2"), sem("x1_in"), sem("eps_set"), sem("w_turned"), sem("w_ready"))
        stats, moments, std, norm_ready = sem("stats2"), sem("moments2"), sem("std2"), sem("norm_ready2")
        z_ready, h_ready, turned, h0t_ready = sem("z_ready"), sem("h_ready2"), sem("turned2"), sem("h0t_ready")
        hi_ready, lo_ready = sem("hi_ready"), sem("lo_ready")
        ed_ready, ed_free, sums_done = sem("ed_ready"), sem("ed_free"), sem("sums_done")
        nh_ready, post_done, bank_free = sem("nh_ready"), sem("post_done"), sem("bank_free")
        col_max, scale_ready, g_ready, g_turned = sem("col_max"), sem("scale_ready"), sem("g_ready"), sem("g_turned")
        ot_ready, ot_turned = sem("ot_ready"), sem("ot_turned")
        xl_in = [sem(f"xl_in{i}") for i in range(4)]
        xl_out = [sem(f"xl_out{i}") for i in range(4)]
        out_q, x1_q = (a.rearrange("(u t b e) d -> b u t e d", u=OCT, t=8, b=PLANES, e=16) for a in (out, x1_dram))
        block = ctx.enter_context(nc.Block())

        @block.sync
        def _(sp):
            sp.dma_start(ID[:], ident).then_inc(consts_in, 16)
            for i, w in enumerate((ws, wn, ws1, wn1)):
                sp.dma_start(WR[:, i, :], w).then_inc(consts_in, 16)
            with nc.sync.Fori(0, PLANES) as b:
                for u in range(OCT):
                    sp.dma_start(X1[:, ds(b * OCT + u, 1), :].squeeze(1), x1_q[b, u]).then_inc(x1_in, 16)

            def load_unit(m):
                for i in range(4):
                    sp.dma_start(XL[:, m % 4, i, :], x1_q[m // 2, m % 2 * 4 + i]).then_inc(xl_in[m % 4], 16)

            for m in range(4):
                load_unit(m)
            for m in range(16):
                sp.wait_ge(bank_free, 24 + m + 1)
                for i in range(4):
                    sp.dma_start(out_q[m // 2, m % 2 * 4 + i], XL[:, m % 4, i, :]).then_inc(xl_out[m % 4], 16)
                if m + 4 < 16:
                    sp.wait_ge(xl_out[m % 4], 64 * (m // 4 + 1))
                    load_unit(m + 4)
            for q in xl_out:
                sp.wait_ge(q, 256)

        @block.tensor
        def _(pe):
            def add_up(R):
                for n in range(NB):
                    pe.wait_ge(ed_ready, R * NB + (n + 1))
                    pe.sem_inc(waited, 1)
                    for part in range(2):
                        for m in range(8):
                            if n == 0 and part == 0:
                                pe.wait_ge(bank_free, R * 8 + (m + 1))
                                pe.sem_inc(waited, 1)
                            edges = ED[:, n % SLOTS, m // 2, m % 2 * 256:m % 2 * 256 + 256].bitcast(F8)
                            mm = pe.matmul(bank[m][:], HS[:, n, part, :], edges,
                                           start=(n == 0 and part == 0), stop=(n == NB - 1 and part == 1))
                            if n == NB - 1 and part == 1 and m < 7:
                                mm.then_inc(sums_done, 1)
                    mm.then_inc(ed_free, 1)

            def combine(R, m, layer, h):
                pe.wait_ge(nh_ready, R * 8 + (m + 1))
                pe.matmul(bank[m][:], WT[:, 2 * layer, :], h, start=True, stop=False)
                pe.matmul(bank[m][:], WT[:, 2 * layer + 1, :], NH[:, m % 2, :], start=False, stop=True) \
                  .then_inc(post_done, 1)

            pe.sem_inc(ed_free, SLOTS)
            pe.sem_inc(post_done, 2)
            pe.sem_inc(turned, 2)
            pe.wait_ge(consts_in, 80)
            for i in range(4):
                t = pe.transpose(bank[7][:, i * P:(i + 1) * P], WR[:, i, :], ID[:])
            t.then_inc(w_turned, 1)
            with nc.tensor.Fori(0, 8) as i:
                for s in range(2):
                    pe.wait_ge(h_ready, i * 2 + (s + 1))
                    pe.wait_ge(h0t_ready, i * 2 + (s + 1))
                    for k in range(4):
                        t = pe.transpose(bank[s][:, k * P:(k + 1) * P], HB[:, s, k * P:(k + 1) * P], ID[:])
                    t.then_inc(turned, 1)
            pe.wait_ge(h0t_ready, 16 + 2)
            pe.wait_ge(w_ready, 1)
            pe.wait_ge(hi_ready, 16 + 2)
            pe.wait_ge(lo_ready, 16 + 2)
            with nc.tensor.Fori(0, 2) as R:
                add_up(R)
                for m in range(8):
                    combine(R, m, 0, H0T[:, ds(R * 4096 + 512 * m, 512)])
            for i in range(16):
                s = i % 2
                pe.wait_ge(g_ready, i + 1)
                if i >= 2:
                    pe.wait_ge(lo_ready, 16 + 2 + i - 1)
                for k in range(4):
                    t = pe.transpose(bank[s][:, k * P:(k + 1) * P], HB[:, s, k * P:(k + 1) * P], ID[:])
                t.then_inc(g_turned, 1)
            pe.wait_ge(hi_ready, 32 + 2)
            pe.wait_ge(lo_ready, 32 + 2)
            with nc.tensor.Fori(2, 4) as R:
                add_up(R)
                for m in range(9):
                    if m < 8:
                        combine(R, m, 1, H1T[:, ds(R * 4096 + (512 * m - 8192), 512)])
                    if m > 0:
                        pe.wait_ge(ot_ready, R * 8 + (m - 16))
                        for k in range(4):
                            t = pe.transpose(bank[m - 1][:, k * P:(k + 1) * P], OT[:, (m - 1) % 2, k * P:(k + 1) * P], ID[:])
                        t.then_inc(ot_turned, 1)

        @block.scalar
        def _(act):
            act.sem_inc(hi_ready, 2)
            act.wait_ge(moments, NB)
            act.wait_ge(eps_set, 1)
            act.activation(RS[:], MV[:, :, 1], ACT.Sqrt, bias=EPSC[:], scale=HSCALE ** -2).then_inc(std, 1)
            with nc.scalar.Fori(0, 8) as i:
                for s in range(2):
                    act.wait_ge(z_ready, i * 2 + (s + 1))
                    act.wait_ge(turned, i * 2 + (s + 1))
                    act.wait_ge(lo_ready, i * 2 + (s + 1))
                    act.activation(HB[:, s, :], ZB[:, s, :], ACT.Relu).then_inc(h_ready, 1)
                    act.activation(HS[:, ds(i * 8 + 4 * s, 4), 0, :], ZB[:, s, :].rearrange("p (k d) -> p k d", d=D),
                                   ACT.Relu).then_inc(hi_ready, 1)

            def neighbours(R, m, scale):
                if m < 7:
                    act.wait_ge(sums_done, R * 7 + (m + 1))
                else:
                    act.wait_ge(ed_free, R * NB + (NB + SLOTS))
                act.wait_ge(post_done, R * 8 + (m + 1))
                act.activation(NH[:, m % 2, :], bank[m][:], ACT.Copy, scale=scale).then_inc(nh_ready, 1)

            with nc.scalar.Fori(0, 2) as R:
                for m in range(8):
                    neighbours(R, m, 0.5)
            for i in range(16):
                act.wait_ge(g_turned, i + 1)
                act.copy(HS[:, 4 * i:4 * i + 4, 0, :], bank[i % 2][:].rearrange("p (k d) -> p k d", d=D)) \
                   .then_inc(hi_ready, 1)
            with nc.scalar.Fori(2, 4) as R:
                for m in range(8):
                    neighbours(R, m, SC[:, 2:3])

        @block.gpsimd
        def _(pool):
            pool.memset(EPSC[:], EPS * HSCALE ** -2).then_inc(eps_set, 1)

        @block.vector
        def _(dve):
            def unpack(R, p, n, slot):
                dve.wait_ge(ed_free, n + (R * NB + 1))
                for i in range(4):
                    b = 4 * p + i
                    op = dve.tensor_scalar(ED[:, slot, i, :].rearrange("p (u w) -> p u w", u=QU),
                                           PK[:, :, ds(n, 1), :].squeeze(2),
                                           abs(6 - b), 0x4040,
                                           ALU.logical_shift_left if b <= 6 else ALU.logical_shift_right,
                                           ALU.bitwise_and)
                op.then_inc(ed_ready, 1)

            dve.sem_inc(bank_free, 8)
            dve.sem_inc(h0t_ready, 2)
            dve.sem_inc(lo_ready, 2)
            dve.wait_ge(x1_in, 16 * NB)
            for qb in range(NB):
                if qb >= 2:
                    dve.wait_ge(moments, qb - 1)
                dve.bn_stats(ST[:, qb % 2, :], X1[:, qb, :]).then_inc(stats, 1)
                if qb >= 1:
                    dve.wait_ge(stats, qb)
                    dve.bn_aggr(MV[:, qb - 1, :], ST[:, (qb - 1) % 2, :]).then_inc(moments, 1)
            dve.wait_ge(stats, NB)
            dve.bn_aggr(MV[:, NB - 1, :], ST[:, (NB - 1) % 2, :]).then_inc(moments, 1)
            dve.wait_ge(w_turned, 1)
            dve.tensor_copy(WT[:].rearrange("p a b -> p (a b)"), bank[7][:]).then_inc(w_ready, 1)
            dve.wait_ge(std, 1)
            dve.reciprocal(RS[:], RS[:]).then_inc(norm_ready, 1)
            dve.wait_ge(norm_ready, 1)
            dve.scalar_tensor_tensor(NM[:], MV[:, :, 0], -1.0, RS[:], ALU.mult, ALU.mult).then_inc(norm_ready, 1)
            dve.wait_ge(norm_ready, 2)

            def normalise(i, s):
                dve.wait_ge(hi_ready, i * 2 + (s + 1))
                for k in range(4):
                    qb = i * 8 + 4 * s + k
                    op = dve.tensor_scalar(ZB[:, s, k * P:(k + 1) * P], X1[:, ds(qb, 1), :].squeeze(1),
                                           RS[:, ds(qb, 1)], NM[:, ds(qb, 1)], ALU.mult, ALU.add)
                op.then_inc(z_ready, 1)

            def finish(i, s):
                dve.wait_ge(hi_ready, i * 2 + (s + 3))
                blocks = ds(i * 8 + 4 * s, 4)
                dve.tensor_tensor(HS[:, blocks, 1, :], HB[:, s, :].rearrange("p (k d) -> p k d", d=D),
                                  HS[:, blocks, 0, :], ALU.subtract).then_inc(lo_ready, 1)
                dve.wait_ge(turned, i * 2 + (s + 3))
                dve.tensor_copy(H0T[:, ds(i * 1024 + 512 * s, 512)], bank[s][:]).then_inc(h0t_ready, 1)

            def unpack_pass(R, first, last):
                with nc.vector.Fori(first, last) as i:
                    for n in range(SLOTS):
                        unpack(R, R % 2, i * SLOTS + n, n)

            def hidden(U):
                if U < 16:
                    dve.wait_ge(post_done, U + 3)
                    dve.tensor_scalar(H1T[:, 512 * U:512 * U + 512], bank[U % 8][:], 1.0 / HSCALE, 0.0,
                                      ALU.mult, ALU.max).then_inc(bank_free, 1)
                if U > 0:
                    dve.wait_ge(bank_free, 8 + U)
                    dve.tensor_reduce(CM[:, U - 1:U], H1T[:, 512 * U - 512:512 * U], AX.X, ALU.max).then_inc(col_max, 1)

            def rows_of_hidden(i):
                if i < 16:
                    if i >= 2:
                        dve.wait_ge(g_turned, i - 1)
                    dve.tensor_scalar(HB[:, i % 2, :], H1T[:, 512 * i:512 * i + 512], SC[:, 1:2], None, ALU.mult) \
                       .then_inc(g_ready, 1)
                if i > 0:
                    j = i - 1
                    dve.wait_ge(hi_ready, 18 + j + 1)
                    dve.tensor_tensor(HS[:, 4 * j:4 * j + 4, 1, :], bank[j % 2][:].rearrange("p (k d) -> p k d", d=D),
                                      HS[:, 4 * j:4 * j + 4, 0, :], ALU.subtract).then_inc(lo_ready, 1)

            def output(v):
                if v >= 2:
                    dve.wait_ge(ot_turned, v - 1)
                dve.wait_ge(post_done, 16 + v + 3)
                dve.tensor_scalar(OT[:, v % 2, :], bank[v % 8][:], 0.0, None, ALU.max).then_inc(ot_ready, 1)

            def result(v):
                dve.wait_ge(ot_turned, v + 1)
                dve.wait_ge(xl_in[v % 4], 64 * (v // 4 + 1))
                xl = XL[:, v % 4].rearrange("p k d -> p (k d)")
                dve.tensor_tensor(xl, xl, bank[v % 8][:], ALU.add).then_inc(bank_free, 1)

            with nc.vector.Fori(0, 8) as i:
                for s in range(2):
                    normalise(i, s)
                for s in range(2):
                    finish(i, s)
            unpack_pass(0, 0, 16)
            unpack_pass(1, 0, 1)
            for U in range(8):
                hidden(U)
            unpack_pass(1, 1, 16)
            unpack_pass(2, 0, 1)
            for U in range(8, 17):
                hidden(U)
            dve.wait_ge(col_max, 16)
            dve.tensor_reduce(SC[:, 0:1], CM[:], AX.X, ALU.max).then_inc(scale_ready, 1)
            dve.wait_ge(scale_ready, 1)
            dve.tensor_scalar(SC[:, 0:1], SC[:, 0:1], TINY, None, ALU.max).then_inc(scale_ready, 1)
            dve.wait_ge(scale_ready, 2)
            dve.reciprocal(SC[:, 1:2], SC[:, 0:1]).then_inc(scale_ready, 1)
            dve.wait_ge(scale_ready, 3)
            dve.tensor_scalar(SC[:, 1:2], SC[:, 1:2], H1MAX, None, ALU.mult).then_inc(scale_ready, 1)
            dve.tensor_scalar(SC[:, 2:3], SC[:, 0:1], 0.5 / H1MAX, None, ALU.mult).then_inc(scale_ready, 1)
            dve.wait_ge(scale_ready, 5)
            for i in range(17):
                rows_of_hidden(i)
            unpack_pass(2, 1, 16)
            unpack_pass(3, 0, 1)
            for R in (2, 3):
                for m in range(9):
                    v = 8 * (R - 2) + m
                    if m < 8:
                        output(v)
                    if m > 0:
                        result(v - 1)
                if R == 2:
                    unpack_pass(3, 1, 16)


def build(nc, x, adj, W, a, ws0, wn0, ws1, wn1, ident, packw, out):
    srow_dram = nc.dram_tensor("srow", (HEADS, N), F32, kind="Internal").ap()
    x1_dram = nc.dram_tensor("x1", (N, D), F32, kind="Internal").ap()
    with ExitStack() as ctx:
        mem = {"PK": ctx.enter_context(nc.sbuf_tensor("PK", [P, QU, NB, QW], U16))}
        with ExitStack() as inner:
            for name, shape, dt in (("X", [P, NB, 2, HEADS, 2 * HC], F16), ("TB", [P, NB, HEADS], F32),
                                    ("NT", [P, NB, HEADS], F32), ("AB", [P, NB, 2 * HEADS], F32),
                                    ("MEAN", [P, D], F32), ("HMAX", [P, 1], F32)):
                mem[name] = inner.enter_context(nc.sbuf_tensor(name, shape, dt))
            input_stage(nc, mem, x, W, a, ident, srow_dram)
            attention_stage(nc, mem, x, adj, packw, srow_dram, x1_dram)
        graph_stage(nc, mem, ident, ws0, wn0, ws1, wn1, x1_dram, out)


_INS = ["x", "adj", "L0_gnn_W", "L0_gnn_a", "L1_gnn_w_self_0", "L1_gnn_w_neigh_0", "L1_gnn_w_self_1",
        "L1_gnn_w_neigh_1"]


def kernel(**inputs):
    import concourse.bacc as bacc
    import ml_dtypes
    from concourse.bass_utils import run_bass_kernel_spmd

    nc = bacc.Bacc("TRN2", target_bir_lowering=False, num_devices=1)
    r = np.arange(P)
    packw = np.zeros((P, 8), np.float32)
    packw[r, r % 16 // 2] = 2.0 ** (r // 16 + 8 * (r % 2))
    arrays = {name: np.ascontiguousarray(inputs[name]) for name in _INS}
    arrays["identity"] = np.eye(P, dtype=np.float32)
    arrays["pack_weights"] = packw.astype(ml_dtypes.bfloat16)
    arrays = {f"in_{n}": v for n, v in arrays.items()}
    args = [nc.dram_tensor(n, v.shape, mybir.dt.from_np(v.dtype), kind="ExternalInput").ap()
            for n, v in arrays.items()]
    out = nc.dram_tensor("out_0", (N, D), F32, kind="ExternalOutput").ap()
    build(nc, *args, out)
    r = run_bass_kernel_spmd(nc, [arrays], core_ids=[0])
    return r.results[0]["out_0"]
```

```python
from contextlib import ExitStack

import numpy as np

import concourse.bass as bass
from concourse import mybir

ALU = mybir.AluOpType
ACT = mybir.ActivationFunctionType
AX = mybir.AxisListType
F32 = mybir.dt.float32
F16 = mybir.dt.float16
BF16 = mybir.dt.bfloat16
F8 = mybir.dt.float8e5
U16 = mybir.dt.uint16
I32 = mybir.dt.int32
RMAX = bass.bass_isa.ReduceOp.max
ds = bass.ds

P = 128
N = 8192
D = 128
NB = N // P
HEADS = 4
HD = D // HEADS
HC = HD + 1
PC = HEADS * HC + 2 * HEADS
PLANES = 8
OCT = NB // PLANES
QW = 8 * P // 16
STRIPS = 4
SW = N // STRIPS
EPS = 1e-5
BIG = 2.0 ** 100
TINY = 1e-30
XSCALE = 2.0 ** 15
LSCALE = 2.0 ** 11
HSCALE = 2.0 ** 12
H1MAX = 2.0 ** 15
SLOTS = 4
EARLY = 1
CHUNK = 8
GROUPS = 2 * OCT
PACKED_GROUPS = GROUPS - 2
BANKW = 462


PACK_AT = {14 * m + step: (m, o) for m in range(4) for o, step in enumerate((0, 1, 2, 4, 5, 7, 8, 10))}
KEEP_AT = {14 * m + 13: m for m in range(4)}
EP = 19
EP_DVE_AT = {2: 0, 4: 1, 6: 2, 8: 3, 10: 4, 12: 5, 14: 6, 16: 7, 34: 11, 35: 12, 36: 13, 37: 14}
EP_POOL_AT = {5: 8, 6: 9, 7: 10, 11: 15, 12: 16, 13: 17, 14: 18}


def act_heads(n):
    return 3 if n % 7 in (1, 4) else 2


M_AT = {}
for _k in range(4):
    M_AT[_k, 0] = (_k, 264)
for _i, _kh in enumerate([(0, 1), (0, 2), (1, 1), (1, 2), (2, 1), (2, 2), (3, 1), (3, 2), (3, 3)]):
    M_AT[_kh] = (4 + _i // 3, 132 * (_i % 3))


def pieces(k):
    out = [(None, (0, 1), k, 0)]
    for h in range(HEADS):
        if (k, h) in M_AT:
            out.append((h, (0, 1), *M_AT[k, h]))
        else:
            out.append((h, (0,), k, 396))
            out.append((h, (1,), 4 + k, 396))
    return out


class Packing:

    def __init__(self, nc, ctx, adj, packw, PK):
        self.nc, self.PK, self.packw = nc, PK, packw
        self.CA = ctx.enter_context(nc.sbuf_tensor("CA", [P, STRIPS, SW], BF16))
        self.PW = ctx.enter_context(nc.sbuf_tensor("PW", [P, 8], BF16))
        self.PKP = ctx.enter_context(nc.psum_tensor("PKP", [P, NB, 8], F32))
        self.strips = adj.rearrange("(t p) (c w) -> t c p w", p=P, w=SW)
        sem = lambda n: ctx.enter_context(nc.semaphore(n))
        self.strip_in = [sem(f"strip_in{c}") for c in range(STRIPS)]
        self.strips_packed = sem("strips_packed")
        self.pk_ready = sem("pk_ready")
        self.weights_in = sem("weights_in")
        self.loads_waited = sem("loads_waited")

    def load_strip(self, pool, T, c):
        pool.wait_ge(self.strips_packed, T * STRIPS + (c + 1))
        pool.sem_inc(self.loads_waited, 1)
        pool.dma_start(self.CA[:, c, :], self.strips[T, c]).then_inc(self.strip_in[c], 16)

    def load_tile(self, pool, T):
        for c in range(STRIPS):
            self.load_strip(pool, T, c)

    def pack(self, pe, T, o):
        if o % 2 == 0:
            pe.wait_ge(self.strip_in[o // 2], T * 16 + 16)
        if o == 0:
            pe.wait_ge(self.pk_ready, T + 1)
        columns = self.CA[:, o // 2, o % 2 * 1024:o % 2 * 1024 + 1024].rearrange("p (q b) -> p b q", b=PLANES)
        for b in range(PLANES):
            mm = pe.matmul(self.PKP[:, o * PLANES + b, :], columns[:, b, :], self.PW[:], start=True, stop=True)
        if o % 2 == 1:
            mm.then_inc(self.strips_packed, 1)

    def keep(self, act, T, u, word):
        act.wait_ge(self.strips_packed, T * STRIPS + 2 * STRIPS)
        act.copy(self.PK[:, ds(u, 1), :, ds(word, 8)].squeeze(1), self.PKP[:]).then_inc(self.pk_ready, 1)


def input_stage(nc, mem, packing, x, W, a, ident, srow_dram):
    X, TB, NT, AB, MEAN, HMAX = mem["X"], mem["TB"], mem["NT"], mem["AB"], mem["MEAN"], mem["HMAX"]
    with ExitStack() as ctx:
        sb = lambda n, s, d: ctx.enter_context(nc.sbuf_tensor(n, s, d))
        ps = lambda n, s: ctx.enter_context(nc.psum_tensor(n, s, F32))
        sem = lambda n: ctx.enter_context(nc.semaphore(n))
        space = mem["PK"][:, 1:OCT].rearrange("p u q w -> p (u q w)").bitcast(F32)
        XQ = space[:, 0:NB * D].rearrange("p (q d) -> p q d", d=D)
        FULL = space[:, NB * D:NB * D + 2 * NB * HC].rearrange("p (i q c) -> p i q c", i=2, c=HC)
        HF = sb("HF", [P, NB, PC], F32)
        MV = sb("MV", [P, NB, 2], F32)
        ST = sb("ST", [P, 4, 6], F32)
        RS = sb("RS", [P, NB], F32)
        NM = sb("NM", [P, NB], F32)
        HB = sb("HB", [P, 2, 4, D], F32)
        HT = sb("HT", [P, 2, 512], F32)
        SR = sb("SR", [HEADS, 2, 512], F32)
        WC = sb("WC", [P, PC], F32)
        WF = sb("WF", [P, HEADS, HD], F32)
        WT = sb("WT", [P, P], F32)
        ABL = sb("ABL", [P, 2 * HEADS], F32)
        ID = sb("ID", [P, P], F32)
        ONES = sb("ONES", [P, P], F32)
        EPSC = sb("EPSC", [P, 1], F32)
        MX = sb("MX", [P, 6], F32)
        MH = sb("MH", [P, 2, 8], F32)
        GM = sb("GM", [P, 6], F32)
        NEGT = sb("NEGT", [P, 8], F32)
        EB = sb("EB", [P, 2, NB, HEADS], F32)
        Y = sb("Y", [P, 2, NB, HEADS], F32)
        YS = sb("YS", [P, NB, HEADS], F32)
        RH = sb("RH", [P, 1], F32)
        PT = ps("PT", [P, 2, 512])
        PP = ps("PP", [P, 4, 512])
        PR = ps("PR", [P, 512])

        x_in = [sem(f"x_in{u}") for u in range(OCT)]
        w_in, w_mem, v_ps, v_sb = sem("w_in"), sem("w_mem"), sem("v_ps"), sem("v_sb")
        stats, moments, std, norm_ready = sem("stats"), sem("moments"), sem("std"), sem("norm_ready")
        h_ready, projected = sem("h_ready"), sem("projected")
        turned = sem("turned")
        ht_ready = sem("ht_ready")
        srows_ps = sem("srows_ps")
        hf_ready = sem("hf_ready")
        sr_ready = sem("sr_ready")
        sr_out = [sem("sr_out0"), sem("sr_out1")]
        maxima, all_max, neg_max, scales = sem("maxima"), sem("all_max"), sem("neg_max"), sem("scales")
        row_args, exps, full, hi_done = sem("row_args"), sem("exps"), sem("full"), sem("hi_done")
        lo_done, mean_ps, largest = sem("lo_done"), sem("mean_ps"), sem("largest")
        x_q = x.rearrange("(u p b) d -> u p b d", u=OCT, b=PLANES)
        block = ctx.enter_context(nc.Block())

        @block.sync
        def _(sp):
            for q in sr_out:
                sp.sem_inc(q, 16)
            for u in range(OCT):
                sp.dma_start(XQ[:, PLANES * u:PLANES * u + PLANES, :], x_q[u]).then_inc(x_in[u], 16)
            sp.dma_start(ID[:], ident).then_inc(w_in, 16)
            sp.dma_start(WF[:], W.rearrange("h i d -> i h d")).then_inc(w_in, 16)
            sp.dma_start(packing.PW[:], packing.packw).then_inc(packing.weights_in, 16)
            sp.wait_ge(w_mem, 2)
            for s in range(2):
                for h in range(HEADS):
                    sp.dma_start(ABL[HD * h:HD * h + HD, HEADS * s + h:HEADS * s + h + 1],
                                 a[h, HD * s:HD * s + HD, :]).then_inc(w_in, 16)
            with nc.sync.Fori(0, 8) as i:
                for s in range(2):
                    sp.wait_ge(sr_ready, i * 2 + (s + 2))
                    sp.dma_start(srow_dram[:, ds(i * 1024 + s * 512, 512)], SR[:, s, :]).then_inc(sr_out[s], 16)
            for q in sr_out:
                sp.wait_ge(q, 128 + 16)

        @block.tensor
        def _(pe):
            def turn(n, s):
                pe.wait_ge(h_ready, n + 1)
                pe.wait_ge(ht_ready, n + 1)
                for k in range(4):
                    mm = pe.transpose(PT[:, s, k * P:(k + 1) * P], HB[:, s, k, :], ID[:])
                mm.then_inc(turned, 1)

            def project(n, s):
                pe.wait_ge(ht_ready, n + 3)
                pe.wait_ge(hf_ready, n * 2 + 1)
                for k in range(4):
                    mm = pe.matmul(PP[:, 2 * s + k // 2, (k % 2) * PC:(k % 2) * PC + PC],
                                   HT[:, s, k * P:(k + 1) * P], WC[:], start=True, stop=True)
                mm.then_inc(projected, 1)
                pe.wait_ge(sr_ready, n + 1)
                pe.matmul(PR[0:HEADS, :], WC[:, PC - HEADS:PC], HT[:, s, :],
                          start=True, stop=True).then_inc(srows_ps, 1)

            pe.sem_inc(turned, 2)
            pe.sem_inc(srows_ps, 2)
            pe.sem_inc(packing.strips_packed, STRIPS)
            pe.wait_ge(w_in, 160)
            pe.transpose(PT[:, 0, 0:P], WF[:].rearrange("p h d -> p (h d)"), ID[:]).then_inc(v_ps, 1)
            pe.wait_ge(v_sb, 1)
            pe.matmul(PT[:, 1, 0:2 * HEADS], WT[:], ABL[:], start=True, stop=True).then_inc(v_ps, 1)
            pe.wait_ge(v_sb, 3)
            pe.wait_ge(packing.weights_in, 16)
            with nc.tensor.Fori(0, 4) as i:
                for pair in range(2):
                    for s in range(2):
                        turn(i * 4 + (2 * pair + s), s)
                    for s in range(2):
                        project(i * 4 + (2 * pair + s), s)
                        for o in range(2):
                            packing.pack(pe, i, 4 * pair + 2 * s + o)
            pe.wait_ge(hf_ready, 2 * 16 + 3)
            for qb in range(NB):
                mm = pe.matmul(PT[:, 0, 0:D], ONES[:],
                               HF[:, qb, 0:HEADS * HC].rearrange("p (h c) -> p h c", c=HC)[:, :, 0:HD],
                               start=(qb == 0), stop=(qb == NB - 1))
                if qb % 16 == 15 and qb < NB - 1:
                    for o in range(8):
                        packing.pack(pe, 4 + qb // 16, o)
            mm.then_inc(mean_ps, 1)
            for o in range(8):
                packing.pack(pe, 7, o)

        @block.scalar
        def _(act):
            act.sem_inc(packing.pk_ready, 1)
            act.wait_ge(moments, NB)
            act.wait_ge(w_mem, 4)
            act.activation(RS[:], MV[:, :, 1], ACT.Sqrt, bias=EPSC[:]).then_inc(std, 1)
            act.wait_ge(norm_ready, 2)
            with nc.scalar.Fori(0, 4) as i:
                for v in range(4):
                    act.wait_ge(turned, i * 4 + (v + 1))
                    for k in range(4):
                        qb = i * 16 + 4 * v + k
                        a_ = act.activation(HB[:, v % 2, k, :], XQ[:, ds(qb, 1), :].squeeze(1), ACT.Relu,
                                            bias=NM[:, ds(qb, 1)], scale=RS[:, ds(qb, 1)])
                    a_.then_inc(h_ready, 1)
                packing.keep(act, i, 0, i * 8)
            packing.keep(act, 4, 0, 32)
            act.wait_ge(neg_max, 2)
            for h in range(HEADS):
                t_h = HF[:, :, HEADS * HC + h]
                act.activation(EB[:, 0, :, h], t_h, ACT.Exp, bias=NEGT[:, h:h + 1]).then_inc(exps, 1)
                act.activation(EB[:, 1, :, h], t_h, ACT.Exp, bias=NEGT[:, 4 + h:5 + h], scale=0.2).then_inc(exps, 1)
            act.wait_ge(row_args, 2)
            for c in range(2):
                act.activation(AB[:].rearrange("p q (h c) -> p q h c", c=2)[:, :, :, c], Y[:, c], ACT.Exp) \
                   .then_inc(exps, 1)
            for j in range(2 * HEADS):
                h, c = j // 2, j % 2
                act.wait_ge(full, j + 1)
                act.activation(X[:, :, 0, h, c * HC:(c + 1) * HC], FULL[:, j % 2], ACT.Copy,
                               scale=1.0 / LSCALE).then_inc(hi_done, 1)
                if j in (2, 4, 6):
                    packing.keep(act, 4 + j // 2, 0, 32 + 4 * j)

        @block.gpsimd
        def _(pool):
            pool.memset(WC[:], 0.0).then_inc(w_mem, 1)
            pool.memset(ABL[:], 0.0).then_inc(w_mem, 1)
            pool.memset(ONES[:], 1.0).then_inc(w_mem, 1)
            pool.memset(EPSC[:], EPS).then_inc(w_mem, 1)
            with nc.gpsimd.Fori(0, 5) as T:
                packing.load_tile(pool, T)
            pool.wait_ge(maxima, 2)
            pool.partition_all_reduce(GM[:], MX[:], P, RMAX).then_inc(all_max, 1)
            with nc.gpsimd.Fori(5, 8) as T:
                packing.load_tile(pool, T)

        @block.vector
        def _(dve):
            dve.sem_inc(ht_ready, 2)
            dve.sem_inc(hf_ready, 3)
            dve.sem_inc(sr_ready, 1)
            for qb in range(NB + 2):
                if qb < NB:
                    if qb % PLANES == 0:
                        dve.wait_ge(x_in[qb // PLANES], 16)
                    if qb >= 4:
                        dve.wait_ge(moments, qb - 3)
                    dve.bn_stats(ST[:, qb % 4, :], XQ[:, qb, :]).then_inc(stats, 1)
                if qb >= 2:
                    dve.wait_ge(stats, qb - 1)
                    dve.bn_aggr(MV[:, qb - 2, :], ST[:, (qb - 2) % 4, :]).then_inc(moments, 1)
            dve.wait_ge(w_mem, 1)
            dve.wait_ge(v_ps, 1)
            dve.tensor_copy(WT[:], PT[:, 0, 0:P]).then_inc(v_sb, 1)
            dve.tensor_copy(WC[:, 0:HEADS * HC].rearrange("p (h c) -> p h c", c=HC)[:, :, 0:HD], WF[:]) \
               .then_inc(v_sb, 1)
            dve.wait_ge(v_ps, 2)
            dve.tensor_copy(WC[:, HEADS * HC:PC], PT[:, 1, 0:2 * HEADS]).then_inc(v_sb, 1)
            dve.wait_ge(std, 1)
            dve.reciprocal(RS[:], RS[:]).then_inc(norm_ready, 1)
            dve.wait_ge(norm_ready, 1)
            dve.scalar_tensor_tensor(NM[:], MV[:, :, 0], -1.0, RS[:], ALU.mult, ALU.mult).then_inc(norm_ready, 1)
            with nc.vector.Fori(0, 8) as i:
                for s in range(2):
                    dve.wait_ge(turned, i * 2 + (s + 3))
                    dve.wait_ge(srows_ps, i * 2 + (s + 1))
                    dve.tensor_copy(HT[:, s, :], PT[:, s, :]).then_inc(ht_ready, 1)
                for s in range(2):
                    dve.wait_ge(projected, i * 2 + (s + 1))
                    for k in range(2):
                        dve.tensor_copy(HF[:, ds(i * 8 + 4 * s + 2 * k, 2), :],
                                        PP[:, 2 * s + k, 0:2 * PC].rearrange("p (k c) -> p k c", c=PC)) \
                           .then_inc(hf_ready, 1)
                    dve.wait_ge(srows_ps, i * 2 + (s + 3))
                    dve.wait_ge(sr_out[s], i * 16 + 16)
                    dve.tensor_copy(SR[:, s, :], PR[0:HEADS, :]).then_inc(sr_ready, 1)
                eight = HF[:, ds(i * 8, 8), 0:HEADS * HC]
                dve.wait_ge(hf_ready, i * 4 + 7)
                dve.tensor_reduce(MH[:, 0, ds(i, 1)], eight, AX.XY, ALU.max).then_inc(largest, 1)
                dve.tensor_reduce(MH[:, 1, ds(i, 1)], eight, AX.XY, ALU.min, negate=True).then_inc(largest, 1)
            dve.wait_ge(hf_ready, 2 * 16 + 3)
            tcol = HF[:, :, HEADS * HC:HEADS * HC + HEADS]
            scol = HF[:, :, PC - HEADS:PC]
            feats = HF[:, :, 0:HEADS * HC]
            dve.tensor_reduce(MX[:, 0:4], tcol.rearrange("p q h -> p h q"), AX.X, ALU.max).then_inc(maxima, 1)
            dve.wait_ge(largest, 16)
            dve.tensor_reduce(MX[:, 4:6], MH[:], AX.X, ALU.max).then_inc(maxima, 1)
            dve.wait_ge(all_max, 1)
            dve.tensor_scalar(NEGT[:, 0:4], GM[:, 0:4], -1.0, None, ALU.mult).then_inc(neg_max, 1)
            dve.tensor_scalar(NEGT[:, 4:8], GM[:, 0:4], -0.2, None, ALU.mult).then_inc(neg_max, 1)
            dve.tensor_scalar(HMAX[:], GM[:, 4:5], GM[:, 5:6], TINY, ALU.max, ALU.max).then_inc(scales, 1)
            dve.tensor_tensor(YS[:], scol, GM[:, 0:4].unsqueeze(1).broadcast_to([P, NB, HEADS]), ALU.add) \
               .then_inc(scales, 1)
            dve.wait_ge(scales, 1)
            dve.reciprocal(RH[:], HMAX[:]).then_inc(scales, 1)
            dve.wait_ge(scales, 2)
            dve.tensor_scalar(Y[:, 0], YS[:], 0.8, 0.0, ALU.mult, ALU.min).then_inc(row_args, 1)
            dve.tensor_scalar(Y[:, 1], YS[:], -0.8, 0.0, ALU.mult, ALU.min).then_inc(row_args, 1)
            dve.tensor_scalar(TB[:], tcol, BIG, None, ALU.mult).then_inc(scales, 1)
            dve.tensor_scalar(NT[:], tcol, -1.0, None, ALU.mult).then_inc(scales, 1)
            dve.wait_ge(exps, 8)
            dve.wait_ge(scales, 3)
            dve.tensor_scalar(EB[:], EB[:], RH[:], XSCALE * LSCALE, ALU.mult, ALU.mult).then_inc(scales, 1)
            dve.tensor_copy(feats.rearrange("p q (h c) -> p q h c", c=HC)[:, :, :, HD],
                            HMAX[:].unsqueeze(2).broadcast_to([P, NB, HEADS])).then_inc(scales, 1)
            dve.wait_ge(scales, 7)
            for j in range(2 * HEADS + 1):
                if j < 2 * HEADS:
                    h, c = j // 2, j % 2
                    if j >= 2:
                        dve.wait_ge(lo_done, j - 1)
                    dve.tensor_tensor(FULL[:, j % 2], HF[:, :, h * HC:(h + 1) * HC],
                                      EB[:, c, :, h].unsqueeze(2).broadcast_to([P, NB, HC]), ALU.mult) \
                       .then_inc(full, 1)
                if j >= 1:
                    h, c = (j - 1) // 2, (j - 1) % 2
                    dve.wait_ge(hi_done, j)
                    dve.scalar_tensor_tensor(X[:, :, 1, h, c * HC:(c + 1) * HC],
                                             X[:, :, 0, h, c * HC:(c + 1) * HC],
                                             -LSCALE, FULL[:, (j - 1) % 2], ALU.mult, ALU.add).then_inc(lo_done, 1)
            dve.wait_ge(mean_ps, 1)
            dve.tensor_scalar(MEAN[:].rearrange("p (h c) -> p h c", c=HD),
                              PT[:, 0, 0:D].rearrange("p (h c) -> p h c", c=HD), 1.0 / N, None, ALU.mult)


def heads_q(v):
    return v.rearrange("(h u p k) d -> u k p h d", h=HEADS, u=OCT, k=2)


def attention_stage(nc, mem, packing, x, srow_dram, x1_dram):
    X, TB, NT, AB, MEAN, HMAX, PK = (mem[n] for n in ("X", "TB", "NT", "AB", "MEAN", "HMAX", "PK"))
    with ExitStack() as ctx:
        sb = lambda n, s, d: ctx.enter_context(nc.sbuf_tensor(n, s, d))
        sem = lambda n: ctx.enter_context(nc.semaphore(n))
        AU = sb("AU", [P, 2, CHUNK, 4, QW], U16)
        MK = sb("MK", [P, SLOTS, HEADS, 512], F8)
        SN = sb("SN", [P, 2, HEADS, 512], F32)
        EV = sb("EV", [P, 7, BANKW], F32)
        MC = sb("MC", [P, 16, 2, HC], F32)
        AC = sb("AC", [P, 16, HC], F32)
        XG = sb("XG", [P, HEADS, 4, HD], F32)
        TM = sb("TM", [P, 16, HD], F32)
        SM = sb("SM", [P, 2, 16], F32)
        acc = [ctx.enter_context(nc.psum_tensor(f"acc{i}", [P, 512], F32)) for i in range(7)]

        waited = sem("waited")
        ep_waited = sem("ep_waited")
        s_in = [sem("s_in0"), sem("s_in1")]
        unpacked = sem("unpacked")
        gt_act, gt_dve = sem("gt_act"), sem("gt_dve")
        masks_ready, masks_free = sem("masks_ready"), sem("masks_free")
        acc_done = sem("acc_done")
        ev_dve, ev_act = sem("ev_dve"), sem("ev_act")
        ep = sem("ep")
        xg_in, x1_out = sem("xg_in"), sem("x1_out")
        block = ctx.enter_context(nc.Block())

        x_q, x1_q = heads_q(x), heads_q(x1_dram)

        def epilogue(eng, g, i):
            eng.wait_ge(ep, g * EP + (i + 1))
            hi_lo = lambda out, hi, lo: eng.scalar_tensor_tensor(out, lo, 1.0 / LSCALE, hi, ALU.mult, ALU.add)
            pair = lambda bank, s0, s1: EV[:, bank, s0 * 132:s1 * 132].rearrange("p (s c x) -> p s c x", c=2, x=66)
            xg = XG[:].rearrange("p h k x -> p k h x")
            MCf = MC[:].rearrange("p m c x -> p m (c x)")
            if i == 0:
                eng.wait_ge(ev_act, g * 3 + 6)
                eng.wait_ge(ev_dve, g * 4 + 8)
            elif i == 16:
                eng.wait_ge(xg_in, g * 16 + 16)
            eng.sem_inc(ep_waited, 1)
            if i == 0:
                op = hi_lo(AC[:].rearrange("p (k h) x -> p k (h x)", k=4), EV[:, 0:4, 0:132], EV[:, 0:4, 132:264])
            elif i == 1:
                op = hi_lo(MCf.rearrange("p (k h) x -> p k h x", k=4)[:, :, 0, :], EV[:, 0:4, 264:330], EV[:, 0:4, 330:396])
            elif i == 2:
                op = hi_lo(MCf.rearrange("p (k h) x -> p k h x", k=4)[:, 0:3, 3, :], EV[:, 0:3, 396:462], EV[:, 4:7, 396:462])
            elif i <= 7:
                bank, s0, s1, m = [(4, 0, 2, 1), (4, 2, 3, 5), (5, 0, 1, 6), (5, 1, 3, 9), (6, 0, 3, 13)][i - 3]
                op = hi_lo(MCf[:, m:m + s1 - s0, :], pair(bank, s0, s1)[:, :, 0, :], pair(bank, s0, s1)[:, :, 1, :])
            elif i == 8:
                op = eng.tensor_tensor(MC[:, :, 1, :], AC[:], MC[:, :, 1, :], ALU.subtract)
            elif i == 9:
                ab = AB[:, ds(g * 4, 4), :].rearrange("p k c -> p (k c)")
                m = MC[:].rearrange("p m c x -> p (m c) x")
                op = eng.tensor_tensor(m, m, ab.unsqueeze(2).broadcast_to([P, 32, HC]), ALU.mult)
            elif i == 10:
                op = eng.tensor_tensor(AC[:], MC[:, :, 0, :], MC[:, :, 1, :], ALU.add)
            elif i == 11:
                op = eng.tensor_scalar(SM[:, 0, :], AC[:, :, HD], 0.0, None, ALU.is_equal)
            elif i == 12:
                op = eng.tensor_tensor(SM[:, 1, :], AC[:, :, HD], SM[:, 0, :], ALU.add)
            elif i == 13:
                op = eng.reciprocal(SM[:, 1, :], SM[:, 1, :])
            elif i == 14:
                op = eng.tensor_scalar(SM[:, 1, :], SM[:, 1, :], HMAX[:], None, ALU.mult)
            elif i == 15:
                op = eng.tensor_tensor(TM[:], AC[:, :, 0:HD], SM[:, 1, :].unsqueeze(2).broadcast_to([P, 16, HD]), ALU.mult)
            elif i == 16:
                op = eng.tensor_tensor(xg, xg, TM[:].rearrange("p (k h) x -> p k h x", k=4), ALU.add)
            elif i == 17:
                mean = MEAN[:].unsqueeze(1).broadcast_to([P, 4, D]).rearrange("p k (h x) -> p k h x", h=HEADS)
                empty = SM[:, 0, :].unsqueeze(2).broadcast_to([P, 16, HD]).rearrange("p (k h) x -> p k h x", k=4)
                op = eng.tensor_tensor(TM[:].rearrange("p (k h) x -> p k h x", k=4), mean, empty, ALU.mult)
            elif i == 18:
                op = eng.tensor_tensor(xg, xg, TM[:].rearrange("p (k h) x -> p k h x", k=4), ALU.add)
            op.then_inc(ep, 1)

        @block.sync
        def _(sp):
            def load_s(g, slot):
                for h in range(HEADS):
                    sp.dma_start(SN[:, slot, h, :], srow_dram[h:h + 1, ds(g * 512, 512)].broadcast_to([P, 512])) \
                      .then_inc(s_in[slot], 16)

            def load_s_after(g, slot):
                sp.wait_ge(gt_act, g * NB + NB)
                sp.wait_ge(gt_dve, g * NB + NB)
                load_s(g + 2, slot)

            def load_x(u, kp):
                sp.dma_start(XG[:].rearrange("p h k x -> p h (k x)"), x_q[u, kp]).then_inc(xg_in, 16)

            def store_x1(u, kp):
                sp.wait_ge(ep, u * (2 * EP) + (kp * EP + EP + 1))
                sp.dma_start(x1_q[u, kp], XG[:].rearrange("p h k x -> p h (k x)")).then_inc(x1_out, 16)

            def swap_x(u, kp):
                store_x1(u, kp)
                sp.wait_ge(x1_out, u * 32 + (kp * 16 + 16))
                load_x(*((u, 1) if kp == 0 else (u + 1, 0)))

            load_s(0, 0)
            load_s(1, 1)
            load_x(0, 0)
            with nc.sync.Fori(0, OCT - 1) as u:
                load_s_after(u * 2, 0)
                swap_x(u, 0)
                load_s_after(u * 2 + 1, 1)
                swap_x(u, 1)
            swap_x(OCT - 1, 0)
            store_x1(OCT - 1, 1)
            sp.wait_ge(x1_out, 16 * GROUPS)

        @block.gpsimd
        def _(pool):
            def tiles(g, last_tile):
                for j in range(4 * STRIPS):
                    if j // STRIPS < last_tile:
                        packing.load_strip(pool, g * 4 + (9 + j // STRIPS), j % STRIPS)
                    if j in EP_POOL_AT:
                        epilogue(pool, g - 1, EP_POOL_AT[j])

            for T in range(8, 13):
                packing.load_tile(pool, T)
            with nc.gpsimd.Fori(1, PACKED_GROUPS - 1) as g:
                tiles(g, 4)
            tiles(PACKED_GROUPS - 1, 3)
            for g in (PACKED_GROUPS, PACKED_GROUPS + 1):
                for i in EP_POOL_AT.values():
                    epilogue(pool, g - 1, i)

        @block.tensor
        def _(pe):
            def group(g, packs):
                for n in range(NB):
                    if packs and n in PACK_AT:
                        m, o = PACK_AT[n]
                        packing.pack(pe, g * 4 + (8 + m), o)
                    pe.wait_ge(masks_ready, g * NB + (n + 1))
                    pe.sem_inc(waited, 1)
                    touched = set()
                    for k in range(4):
                        for h, parts, bank, col in pieces(k):
                            if n == 0 and bank not in touched:
                                if bank < 4:
                                    pe.wait_ge(ev_dve, g * 4 + (bank + 1))
                                else:
                                    pe.wait_ge(ev_act, g * 3 + (bank - 3))
                                pe.sem_inc(waited, 1)
                            lo, hi = parts[0], parts[-1] + 1
                            if h is None:
                                lhs = AU[:, n // CHUNK % 2, n % CHUNK, k, :].bitcast(F8)
                                rhs = X[:, n, :, :, HC:2 * HC]
                            else:
                                lhs = MK[:, n % SLOTS, h, k * P:(k + 1) * P]
                                rhs = X[:, n, lo:hi, h, :]
                            width = 66 * (hi - lo) * (HEADS // 2 if h is None else 1)
                            mm = pe.matmul(acc[bank][:, col:col + width], lhs, rhs,
                                           start=(n == 0 and bank not in touched), stop=(n == NB - 1),
                                           skip_group_check=True)
                            touched.add(bank)
                        if n == NB - 1 and k < 3:
                            mm.then_inc(acc_done, 1)
                    mm.then_inc(masks_free, 1)

            pe.sem_inc(masks_free, SLOTS)
            with nc.tensor.Fori(0, PACKED_GROUPS) as g:
                group(g, True)
            with nc.tensor.Fori(PACKED_GROUPS, GROUPS) as g:
                group(g, False)

        @block.scalar
        def _(act):
            def compare(u, kp, n):
                if n == 0:
                    act.wait_ge(s_in[kp], u * 64 + 64)
                act.wait_ge(masks_free, u * (2 * NB) + (kp * NB + n + 1))
                act.sem_inc(waited, 1)
                for h in range(act_heads(n)):
                    c = act.activation(MK[:, n % SLOTS, h, :], SN[:, kp, h, :], ACT.Relu, bias=TB[:, n, h:h + 1],
                                       scale=BIG, saturate=False)
                c.then_inc(gt_act, 1)

            def start(u, kp):
                for n in range(EARLY + 1):
                    compare(u, kp, n)

            def steps(u, kp, packs):
                for n in range(EARLY + 1, NB):
                    compare(u, kp, n)
                    if packs and n in KEEP_AT:
                        t = 4 * kp + KEEP_AT[n]
                        packing.keep(act, u * 8 + (8 + t), u + 1, 8 * t)

            def copy_acc(u, kp):
                g = u * 2 + kp
                act.wait_ge(ep, g * EP + 1)
                for bank, done in ((4, 2), (5, 3)):
                    act.wait_ge(acc_done, g * 3 + done)
                    act.copy(EV[:, bank, :], acc[bank][:, 0:BANKW]).then_inc(ev_act, 1)
                act.wait_ge(masks_free, g * NB + (NB + SLOTS))
                act.copy(EV[:, 6, :], acc[6][:, 0:BANKW]).then_inc(ev_act, 1)

            act.sem_inc(ev_act, 3)
            start(0, 0)
            with nc.scalar.Fori(0, OCT - 1) as u:
                for kp in range(2):
                    steps(u, kp, True)
                    start(*((u, 1) if kp == 0 else (u + 1, 0)))
                    copy_acc(u, kp)
            for kp in range(2):
                steps(OCT - 1, kp, False)
                if kp == 0:
                    start(OCT - 1, 1)
                copy_acc(OCT - 1, kp)

        @block.vector
        def _(dve):
            def unpack(u, kp, q, r):
                b = 4 * kp + r
                if q > 0 or kp > 0 or not isinstance(u, int):
                    dve.wait_ge(masks_free, u * (2 * NB) + (kp * NB + q * CHUNK - CHUNK + SLOTS))
                dve.tensor_scalar(AU[:, q % 2, :, r, :], PK[:, ds(u, 1), CHUNK * q:CHUNK * q + CHUNK, :].squeeze(1),
                                  abs(6 - b), 0x4040,
                                  ALU.logical_shift_left if b <= 6 else ALU.logical_shift_right,
                                  ALU.bitwise_and).then_inc(unpacked, 1)

            def compare(u, kp, n):
                if n == 0:
                    dve.wait_ge(s_in[kp], u * 64 + 64)
                dve.wait_ge(masks_free, u * (2 * NB) + (kp * NB + n + 1))
                dve.sem_inc(waited, 1)
                for h in range(act_heads(n), HEADS):
                    c = dve.tensor_scalar(MK[:, n % SLOTS, h, :], SN[:, kp, h, :], NT[:, n, h:h + 1], 2.0,
                                          ALU.is_gt, ALU.mult, saturate=False)
                c.then_inc(gt_dve, 1)

            def mask(u, kp, n):
                S = u * (2 * NB) + (kp * NB + n)
                if n % CHUNK == 0:
                    dve.wait_ge(unpacked, u * 64 + (kp * 32 + n // CHUNK * 4 + 4))
                dve.wait_ge(gt_dve, S + 1)
                dve.wait_ge(gt_act, S + 1)
                m = MK[:, n % SLOTS].bitcast(U16)
                edges = AU[:, n // CHUNK % 2, n % CHUNK].rearrange("p r w -> p (r w)")
                dve.tensor_tensor(m, m, edges.unsqueeze(1).broadcast_to([P, HEADS, 4 * QW]), ALU.bitwise_and) \
                   .then_inc(masks_ready, 1)

            def start(u, kp):
                if kp == 0:
                    dve.wait_ge(packing.pk_ready, u * 8 + 9)
                for r in range(4):
                    unpack(u, kp, 0, r)
                compare(u, kp, 0)
                for n in range(EARLY):
                    mask(u, kp, n)
                    compare(u, kp, n + 1)

            def copy_acc(u, kp):
                g = u * 2 + kp
                dve.wait_ge(ep, g * EP + 1)
                for k in range(3):
                    dve.wait_ge(acc_done, g * 3 + (k + 1))
                    dve.tensor_copy(EV[:, k, :], acc[k][:, 0:BANKW]).then_inc(ev_dve, 1)
                dve.wait_ge(masks_free, g * NB + (NB + SLOTS))
                dve.tensor_copy(EV[:, 3, 0:396], acc[3][:, 0:396]).then_inc(ev_dve, 1)

            def step(u, kp, n):
                if n >= EARLY:
                    mask(u, kp, n)
                    if n < NB - 1:
                        compare(u, kp, n + 1)
                if n % CHUNK in (3, 4, 5, 6) and n // CHUNK + 1 < NB // CHUNK:
                    unpack(u, kp, n // CHUNK + 1, n % CHUNK - 3)

            dve.sem_inc(ev_dve, 4)
            dve.sem_inc(ep, 1)
            start(0, 0)
            for n in range(NB):
                step(0, 0, n)
            start(0, 1)
            copy_acc(0, 0)
            with nc.vector.Fori(0, OCT - 1) as u:
                for nu, nkp in ((u, 1), (u + 1, 0)):
                    for n in range(NB):
                        step(nu, nkp, n)
                        if n in EP_DVE_AT:
                            epilogue(dve, u * 2 + (1 - nkp), EP_DVE_AT[n])
                    start(*((nu, 1) if nkp == 0 else (nu + 1, 0)))
                    copy_acc(nu, nkp)
            for n in range(NB):
                step(OCT - 1, 1, n)
                if n in EP_DVE_AT:
                    epilogue(dve, GROUPS - 2, EP_DVE_AT[n])
            copy_acc(OCT - 1, 1)
            for i in range(EP):
                epilogue(dve, GROUPS - 1, i)


def graph_stage(nc, mem, ident, ws, wn, ws1, wn1, x1_dram, out):
    PK = mem["PK"]
    with ExitStack() as ctx:
        sb = lambda n, s, d: ctx.enter_context(nc.sbuf_tensor(n, s, d))
        sem = lambda n: ctx.enter_context(nc.semaphore(n))
        HS = sb("HS", [P, NB, 2, D], F16)
        H0T = sb("H0T", [P, N], F32)
        H1T = sb("H1T", [P, N], F32)
        X1 = H1T[:].rearrange("p (q d) -> p q d", d=D)
        ED = sb("ED", [P, SLOTS, 4, PLANES, QW], U16)
        WR = sb("WR", [P, 4, P], F32)
        WT = sb("WTT", [P, 4, P], F32)
        ID = sb("ID2", [P, P], F32)
        MV = sb("MV2", [P, NB, 2], F32)
        ST = sb("ST2", [P, 4, 6], F32)
        RS = sb("RS2", [P, NB], F32)
        NM = sb("NM2", [P, NB], F32)
        EPSC = sb("EPSC2", [P, 1], F32)
        ZB = sb("ZB", [P, 2, 512], F32)
        HB = sb("HB2", [P, 2, 512], F32)
        NH = sb("NH", [P, 2, 512], F32)
        OT = sb("OT", [P, 2, 512], F32)
        XL = sb("XL", [P, 4, 4, D], F32)
        CM = sb("CM", [P, 16], F32)
        SC = sb("SC", [P, 3], F32)
        bank = [ctx.enter_context(nc.psum_tensor(f"bank{i}", [P, 512], F32)) for i in range(8)]

        waited = sem("waited2")
        x1_in = [sem(f"x1_in{u}") for u in range(OCT)]
        consts_in, eps_set, w_turned, w_ready = (
            sem("consts_in2"), sem("eps_set"), sem("w_turned"), sem("w_ready"))
        stats, moments, std, norm_ready = sem("stats2"), sem("moments2"), sem("std2"), sem("norm_ready2")
        z_ready, h_ready, turned, h0t_ready = sem("z_ready"), sem("h_ready2"), sem("turned2"), sem("h0t_ready")
        hi_ready, lo_ready = sem("hi_ready"), sem("lo_ready")
        ed_ready, ed_free, sums_done = sem("ed_ready"), sem("ed_free"), sem("sums_done")
        nh_ready, post_done, bank_free = sem("nh_ready"), sem("post_done"), sem("bank_free")
        col_max, scale_ready, g_ready, g_turned = sem("col_max"), sem("scale_ready"), sem("g_ready"), sem("g_turned")
        ot_ready, ot_turned = sem("ot_ready"), sem("ot_turned")
        xl_in = [sem(f"xl_in{i}") for i in range(4)]
        xl_out = [sem(f"xl_out{i}") for i in range(4)]
        x1_q = x1_dram.rearrange("(u p b) d -> u p b d", u=OCT, b=PLANES)
        out_u, x1_u = (v.rearrange("(u p c b) d -> u c p b d", u=OCT, c=2, b=4) for v in (out, x1_dram))
        block = ctx.enter_context(nc.Block())

        @block.sync
        def _(sp):
            sp.dma_start(ID[:], ident).then_inc(consts_in, 16)
            for i, w in enumerate((ws, wn, ws1, wn1)):
                sp.dma_start(WR[:, i, :], w).then_inc(consts_in, 16)
            for u in range(OCT):
                sp.dma_start(X1[:, PLANES * u:PLANES * u + PLANES, :], x1_q[u]).then_inc(x1_in[u], 16)

            def load_unit(m):
                sp.dma_start(XL[:, m % 4], x1_u[m // 2, m % 2]).then_inc(xl_in[m % 4], 16)

            for m in range(4):
                load_unit(m)
            for m in range(16):
                sp.wait_ge(bank_free, 24 + m + 1)
                sp.dma_start(out_u[m // 2, m % 2], XL[:, m % 4]).then_inc(xl_out[m % 4], 16)
                if m + 4 < 16:
                    sp.wait_ge(xl_out[m % 4], 16 * (m // 4 + 1))
                    load_unit(m + 4)
            for q in xl_out:
                sp.wait_ge(q, 64)

        @block.tensor
        def _(pe):
            def add_up(R):
                for n in range(NB):
                    pe.wait_ge(ed_ready, R * NB + (n + 1))
                    pe.sem_inc(waited, 1)
                    for part in range(2):
                        for m in range(8):
                            if n == 0 and part == 0:
                                pe.wait_ge(bank_free, R * 8 + (m + 1))
                                pe.sem_inc(waited, 1)
                            edges = ED[:, n % SLOTS, m // 2, m % 2 * 4:m % 2 * 4 + 4, :].rearrange("p b w -> p (b w)").bitcast(F8)
                            mm = pe.matmul(bank[m][:], HS[:, n, part, :], edges,
                                           start=(n == 0 and part == 0), stop=(n == NB - 1 and part == 1))
                            if n == NB - 1 and part == 1 and m < 7:
                                mm.then_inc(sums_done, 1)
                    mm.then_inc(ed_free, 1)

            def combine(R, m, layer, h):
                pe.wait_ge(nh_ready, R * 8 + (m + 1))
                pe.matmul(bank[m][:], WT[:, 2 * layer, :], h, start=True, stop=False)
                pe.matmul(bank[m][:], WT[:, 2 * layer + 1, :], NH[:, m % 2, :], start=False, stop=True) \
                  .then_inc(post_done, 1)

            pe.sem_inc(ed_free, SLOTS)
            pe.sem_inc(post_done, 2)
            pe.sem_inc(turned, 2)
            pe.wait_ge(consts_in, 80)
            for i in range(4):
                t = pe.transpose(bank[7][:, i * P:(i + 1) * P], WR[:, i, :], ID[:])
            t.then_inc(w_turned, 1)
            with nc.tensor.Fori(0, 8) as i:
                for s in range(2):
                    pe.wait_ge(h_ready, i * 2 + (s + 1))
                    pe.wait_ge(h0t_ready, i * 2 + (s + 1))
                    for k in range(4):
                        t = pe.transpose(bank[s][:, k * P:(k + 1) * P], HB[:, s, k * P:(k + 1) * P], ID[:])
                    t.then_inc(turned, 1)
            pe.wait_ge(h0t_ready, 16 + 2)
            pe.wait_ge(w_ready, 1)
            pe.wait_ge(hi_ready, 16 + 2)
            pe.wait_ge(lo_ready, 16 + 2)
            with nc.tensor.Fori(0, 2) as R:
                add_up(R)
                for m in range(8):
                    combine(R, m, 0, H0T[:, ds(R * 4096 + 512 * m, 512)])
            for i in range(16):
                s = i % 2
                pe.wait_ge(g_ready, i + 1)
                if i >= 2:
                    pe.wait_ge(lo_ready, 16 + 2 + i - 1)
                for k in range(4):
                    t = pe.transpose(bank[s][:, k * P:(k + 1) * P], HB[:, s, k * P:(k + 1) * P], ID[:])
                t.then_inc(g_turned, 1)
            pe.wait_ge(hi_ready, 32 + 2)
            pe.wait_ge(lo_ready, 32 + 2)
            with nc.tensor.Fori(2, 4) as R:
                add_up(R)
                for m in range(9):
                    if m < 8:
                        combine(R, m, 1, H1T[:, ds(R * 4096 + (512 * m - 8192), 512)])
                    if m > 0:
                        pe.wait_ge(ot_ready, R * 8 + (m - 16))
                        for k in range(4):
                            t = pe.transpose(bank[m - 1][:, k * P:(k + 1) * P], OT[:, (m - 1) % 2, k * P:(k + 1) * P], ID[:])
                        t.then_inc(ot_turned, 1)

        @block.scalar
        def _(act):
            act.sem_inc(hi_ready, 2)
            act.wait_ge(moments, NB)
            act.wait_ge(eps_set, 1)
            act.activation(RS[:], MV[:, :, 1], ACT.Sqrt, bias=EPSC[:], scale=HSCALE ** -2).then_inc(std, 1)
            with nc.scalar.Fori(0, 8) as i:
                for s in range(2):
                    act.wait_ge(z_ready, i * 2 + (s + 1))
                    act.wait_ge(turned, i * 2 + (s + 1))
                    act.wait_ge(lo_ready, i * 2 + (s + 1))
                    act.activation(HB[:, s, :], ZB[:, s, :], ACT.Relu).then_inc(h_ready, 1)
                    act.activation(HS[:, ds(i * 8 + 4 * s, 4), 0, :], ZB[:, s, :].rearrange("p (k d) -> p k d", d=D),
                                   ACT.Relu).then_inc(hi_ready, 1)

            def neighbours(R, m, scale):
                if m < 7:
                    act.wait_ge(sums_done, R * 7 + (m + 1))
                else:
                    act.wait_ge(ed_free, R * NB + (NB + SLOTS))
                act.wait_ge(post_done, R * 8 + (m + 1))
                act.activation(NH[:, m % 2, :], bank[m][:], ACT.Copy, scale=scale).then_inc(nh_ready, 1)

            with nc.scalar.Fori(0, 2) as R:
                for m in range(8):
                    neighbours(R, m, 0.5)
            for i in range(16):
                act.wait_ge(g_turned, i + 1)
                act.copy(HS[:, 4 * i:4 * i + 4, 0, :], bank[i % 2][:].rearrange("p (k d) -> p k d", d=D)) \
                   .then_inc(hi_ready, 1)
            with nc.scalar.Fori(2, 4) as R:
                for m in range(8):
                    neighbours(R, m, SC[:, 2:3])

        @block.gpsimd
        def _(pool):
            pool.memset(EPSC[:], EPS * HSCALE ** -2).then_inc(eps_set, 1)

        @block.vector
        def _(dve):
            def unpack(R, p, n, slot):
                dve.wait_ge(ed_free, n + (R * NB + 1))
                for b in range(PLANES):
                    op = dve.tensor_scalar(ED[:, slot, :, b, :], PK[:, 4 * p:4 * p + 4, ds(n, 1), :].squeeze(2),
                                           abs(6 - b), 0x4040,
                                           ALU.logical_shift_left if b <= 6 else ALU.logical_shift_right,
                                           ALU.bitwise_and)
                op.then_inc(ed_ready, 1)

            dve.sem_inc(bank_free, 8)
            dve.sem_inc(h0t_ready, 2)
            dve.sem_inc(lo_ready, 2)
            for qb in range(NB + 2):
                if qb < NB:
                    if qb % PLANES == 0:
                        dve.wait_ge(x1_in[qb // PLANES], 16)
                    if qb >= 4:
                        dve.wait_ge(moments, qb - 3)
                    dve.bn_stats(ST[:, qb % 4, :], X1[:, qb, :]).then_inc(stats, 1)
                if qb >= 2:
                    dve.wait_ge(stats, qb - 1)
                    dve.bn_aggr(MV[:, qb - 2, :], ST[:, (qb - 2) % 4, :]).then_inc(moments, 1)
            dve.wait_ge(w_turned, 1)
            dve.tensor_copy(WT[:].rearrange("p a b -> p (a b)"), bank[7][:]).then_inc(w_ready, 1)
            dve.wait_ge(std, 1)
            dve.reciprocal(RS[:], RS[:]).then_inc(norm_ready, 1)
            dve.wait_ge(norm_ready, 1)
            dve.scalar_tensor_tensor(NM[:], MV[:, :, 0], -1.0, RS[:], ALU.mult, ALU.mult).then_inc(norm_ready, 1)
            dve.wait_ge(norm_ready, 2)

            def normalise(i, s):
                dve.wait_ge(hi_ready, i * 2 + (s + 1))
                for k in range(4):
                    qb = i * 8 + 4 * s + k
                    op = dve.tensor_scalar(ZB[:, s, k * P:(k + 1) * P], X1[:, ds(qb, 1), :].squeeze(1),
                                           RS[:, ds(qb, 1)], NM[:, ds(qb, 1)], ALU.mult, ALU.add)
                op.then_inc(z_ready, 1)

            def finish(i, s):
                dve.wait_ge(hi_ready, i * 2 + (s + 3))
                blocks = ds(i * 8 + 4 * s, 4)
                dve.tensor_tensor(HS[:, blocks, 1, :], HB[:, s, :].rearrange("p (k d) -> p k d", d=D),
                                  HS[:, blocks, 0, :], ALU.subtract).then_inc(lo_ready, 1)
                dve.wait_ge(turned, i * 2 + (s + 3))
                dve.tensor_copy(H0T[:, ds(i * 1024 + 512 * s, 512)], bank[s][:]).then_inc(h0t_ready, 1)

            def unpack_pass(R, first, last):
                with nc.vector.Fori(first, last) as i:
                    for n in range(SLOTS):
                        unpack(R, R % 2, i * SLOTS + n, n)

            def hidden(U):
                if U < 16:
                    dve.wait_ge(post_done, U + 3)
                    dve.tensor_scalar(H1T[:, 512 * U:512 * U + 512], bank[U % 8][:], 1.0 / HSCALE, 0.0,
                                      ALU.mult, ALU.max).then_inc(bank_free, 1)
                if U > 0:
                    dve.wait_ge(bank_free, 8 + U)
                    dve.tensor_reduce(CM[:, U - 1:U], H1T[:, 512 * U - 512:512 * U], AX.X, ALU.max).then_inc(col_max, 1)

            def rows_of_hidden(i):
                if i < 16:
                    if i >= 2:
                        dve.wait_ge(g_turned, i - 1)
                    dve.tensor_scalar(HB[:, i % 2, :], H1T[:, 512 * i:512 * i + 512], SC[:, 1:2], None, ALU.mult) \
                       .then_inc(g_ready, 1)
                if i > 0:
                    j = i - 1
                    dve.wait_ge(hi_ready, 18 + j + 1)
                    dve.tensor_tensor(HS[:, 4 * j:4 * j + 4, 1, :], bank[j % 2][:].rearrange("p (k d) -> p k d", d=D),
                                      HS[:, 4 * j:4 * j + 4, 0, :], ALU.subtract).then_inc(lo_ready, 1)

            def output(v):
                if v >= 2:
                    dve.wait_ge(ot_turned, v - 1)
                dve.wait_ge(post_done, 16 + v + 3)
                dve.tensor_scalar(OT[:, v % 2, :], bank[v % 8][:], 0.0, None, ALU.max).then_inc(ot_ready, 1)

            def result(v):
                dve.wait_ge(ot_turned, v + 1)
                dve.wait_ge(xl_in[v % 4], 16 * (v // 4 + 1))
                xl = XL[:, v % 4].rearrange("p k d -> p (k d)")
                dve.tensor_tensor(xl, xl, bank[v % 8][:], ALU.add).then_inc(bank_free, 1)

            for s in range(2):
                normalise(0, s)
            with nc.vector.Fori(0, 7) as i:
                for s in range(2):
                    normalise(i + 1, s)
                    finish(i, s)
            for s in range(2):
                finish(7, s)
            unpack_pass(0, 0, 16)
            unpack_pass(1, 0, 1)
            for U in range(8):
                hidden(U)
            unpack_pass(1, 1, 16)
            unpack_pass(2, 0, 1)
            for U in range(8, 17):
                hidden(U)
            dve.wait_ge(col_max, 16)
            dve.tensor_reduce(SC[:, 0:1], CM[:], AX.X, ALU.max).then_inc(scale_ready, 1)
            dve.wait_ge(scale_ready, 1)
            dve.tensor_scalar(SC[:, 0:1], SC[:, 0:1], TINY, None, ALU.max).then_inc(scale_ready, 1)
            dve.wait_ge(scale_ready, 2)
            dve.reciprocal(SC[:, 1:2], SC[:, 0:1]).then_inc(scale_ready, 1)
            dve.wait_ge(scale_ready, 3)
            dve.tensor_scalar(SC[:, 1:2], SC[:, 1:2], H1MAX, None, ALU.mult).then_inc(scale_ready, 1)
            dve.tensor_scalar(SC[:, 2:3], SC[:, 0:1], 0.5 / H1MAX, None, ALU.mult).then_inc(scale_ready, 1)
            dve.wait_ge(scale_ready, 5)
            for i in range(17):
                rows_of_hidden(i)
            unpack_pass(2, 1, 16)
            unpack_pass(3, 0, 1)
            for R in (2, 3):
                for m in range(9):
                    v = 8 * (R - 2) + m
                    if m < 8:
                        output(v)
                    if m > 0:
                        result(v - 1)
                if R == 2:
                    unpack_pass(3, 1, 16)


def build(nc, x, adj, W, a, ws0, wn0, ws1, wn1, ident, packw, out):
    srow_dram = nc.dram_tensor("srow", (HEADS, N), F32, kind="Internal").ap()
    x1_dram = nc.dram_tensor("x1", (N, D), F32, kind="Internal").ap()
    with ExitStack() as ctx:
        mem = {"PK": ctx.enter_context(nc.sbuf_tensor("PK", [P, OCT, NB, QW], U16))}
        with ExitStack() as inner:
            for name, shape, dt in (("X", [P, NB, 2, HEADS, 2 * HC], F16), ("TB", [P, NB, HEADS], F32),
                                    ("NT", [P, NB, HEADS], F32), ("AB", [P, NB, 2 * HEADS], F32),
                                    ("MEAN", [P, D], F32), ("HMAX", [P, 1], F32)):
                mem[name] = inner.enter_context(nc.sbuf_tensor(name, shape, dt))
            packing = Packing(nc, inner, adj, packw, mem["PK"])
            input_stage(nc, mem, packing, x, W, a, ident, srow_dram)
            attention_stage(nc, mem, packing, x, srow_dram, x1_dram)
        graph_stage(nc, mem, ident, ws0, wn0, ws1, wn1, x1_dram, out)


_INS = ["x", "adj", "L0_gnn_W", "L0_gnn_a", "L1_gnn_w_self_0", "L1_gnn_w_neigh_0", "L1_gnn_w_self_1",
        "L1_gnn_w_neigh_1"]


def kernel(**inputs):
    import concourse.bacc as bacc
    import ml_dtypes
    from concourse.bass_utils import run_bass_kernel_spmd

    nc = bacc.Bacc("TRN2", target_bir_lowering=False, num_devices=1)
    r = np.arange(P)
    packw = np.zeros((P, 8), np.float32)
    packw[r, r // 16] = 2.0 ** (r % 8 + 8 * (r // 8 % 2))
    arrays = {name: np.ascontiguousarray(inputs[name]) for name in _INS}
    arrays["identity"] = np.eye(P, dtype=np.float32)
    arrays["pack_weights"] = packw.astype(ml_dtypes.bfloat16)
    arrays = {f"in_{n}": v for n, v in arrays.items()}
    args = [nc.dram_tensor(n, v.shape, mybir.dt.from_np(v.dtype), kind="ExternalInput").ap()
            for n, v in arrays.items()]
    out = nc.dram_tensor("out_0", (N, D), F32, kind="ExternalOutput").ap()
    build(nc, *args, out)
    r = run_bass_kernel_spmd(nc, [arrays], core_ids=[0])
    return r.results[0]["out_0"]
```

```python
from contextlib import ExitStack

import numpy as np

import concourse.bass as bass
from concourse import mybir

ALU = mybir.AluOpType
ACT = mybir.ActivationFunctionType
AX = mybir.AxisListType
F32 = mybir.dt.float32
F16 = mybir.dt.float16
BF16 = mybir.dt.bfloat16
F8 = mybir.dt.float8e5
U16 = mybir.dt.uint16
RMAX = bass.bass_isa.ReduceOp.max
ds = bass.ds

P = 128
N = 8192
D = 128
NB = N // P
HEADS = 4
HD = D // HEADS
HC = HD + 1
PC = HEADS * HC + 2 * HEADS
PLANES = 8
OCT = NB // PLANES
QW = 8 * P // 16
STRIPS = 4
SW = N // STRIPS
EPS = 1e-5
BIG = 2.0 ** 100
TINY = 1e-30
XSCALE = 2.0 ** 15
LSCALE = 2.0 ** 11
HSCALE = 2.0 ** 12
H1MAX = 2.0 ** 15
SLOTS = 4
EARLY = 1
CHUNK = 8
GROUPS = 2 * OCT
PACKED_GROUPS = GROUPS - 2
BANKW = 462
PACK_AT = {15 * m + step: (m, o) for m in range(4) for o, step in enumerate((0, 2, 4, 6, 8, 10, 12, 13))}
KEEP_AT = {15 * m + 15: m for m in range(4)}
EP = 19
EP_DVE_AT = {2: 0, 4: 1, 6: 2, 8: 3, 10: 4, 12: 5, 14: 6, 16: 7, 34: 11, 35: 12, 36: 13, 37: 14}
EP_POOL_AT = {5: 8, 6: 9, 7: 10, 10: 15, 11: 16, 12: 17, 13: 18}


def act_heads(n):
    return 3 if n % 7 in (1, 4) else 2


M_AT = {}
for _k in range(4):
    M_AT[_k, 0] = (_k, 264)
for _i, _kh in enumerate([(0, 1), (0, 2), (1, 1), (1, 2), (2, 1), (2, 2), (3, 1), (3, 2), (3, 3)]):
    M_AT[_kh] = (4 + _i // 3, 132 * (_i % 3))


def pieces(k):
    out = [(None, (0, 1), k, 0)]
    for h in range(HEADS):
        if (k, h) in M_AT:
            out.append((h, (0, 1), *M_AT[k, h]))
        else:
            out.append((h, (0,), k, 396))
            out.append((h, (1,), 4 + k, 396))
    return out


class Packing:

    def __init__(self, nc, ctx, adj, packw, PK):
        self.nc, self.PK, self.packw = nc, PK, packw
        self.CA = ctx.enter_context(nc.sbuf_tensor("CA", [P, STRIPS, SW], BF16))
        self.PW = ctx.enter_context(nc.sbuf_tensor("PW", [P, 8], BF16))
        self.PKP = ctx.enter_context(nc.psum_tensor("PKP", [P, NB, 8], F32))
        self.strips = adj.rearrange("(t p) (c w) -> t c p w", p=P, w=SW)
        sem = lambda n: ctx.enter_context(nc.semaphore(n))
        self.strip_in = [sem(f"strip_in{c}") for c in range(STRIPS)]
        self.strips_packed = sem("strips_packed")
        self.pk_ready = sem("pk_ready")
        self.weights_in = sem("weights_in")
        self.loads_waited = sem("loads_waited")

    def load_strip(self, pool, T, c):
        pool.wait_ge(self.strips_packed, T * STRIPS + (c + 1))
        pool.sem_inc(self.loads_waited, 1)
        pool.dma_start(self.CA[:, c, :], self.strips[T, c]).then_inc(self.strip_in[c], 16)

    def load_tile(self, pool, T):
        for c in range(STRIPS):
            self.load_strip(pool, T, c)

    def pack(self, pe, T, o):
        if o % 2 == 0:
            pe.wait_ge(self.strip_in[o // 2], T * 16 + 16)
        if o == 0:
            pe.wait_ge(self.pk_ready, T + 1)
        columns = self.CA[:, o // 2, o % 2 * 1024:o % 2 * 1024 + 1024].rearrange("p (q b) -> p b q", b=PLANES)
        for b in range(PLANES):
            mm = pe.matmul(self.PKP[:, o * PLANES + b, :], columns[:, b, :], self.PW[:], start=True, stop=True)
        if o % 2 == 1:
            mm.then_inc(self.strips_packed, 1)

    def keep(self, act, T, u, word):
        act.wait_ge(self.strips_packed, T * STRIPS + 2 * STRIPS)
        act.copy(self.PK[:, ds(u, 1), :, ds(word, 8)].squeeze(1), self.PKP[:]).then_inc(self.pk_ready, 1)


def input_stage(nc, mem, packing, x, W, a, ident, srow_dram):
    X, TB, NT, AB, MEAN, HMAX = mem["X"], mem["TB"], mem["NT"], mem["AB"], mem["MEAN"], mem["HMAX"]
    with ExitStack() as ctx:
        sb = lambda n, s, d: ctx.enter_context(nc.sbuf_tensor(n, s, d))
        ps = lambda n, s: ctx.enter_context(nc.psum_tensor(n, s, F32))
        sem = lambda n: ctx.enter_context(nc.semaphore(n))
        space = mem["PK"][:, 1:OCT].rearrange("p u q w -> p (u q w)").bitcast(F32)
        XQ = space[:, 0:NB * D].rearrange("p (q d) -> p q d", d=D)
        FULL = space[:, NB * D:NB * D + 2 * NB * HC].rearrange("p (i q c) -> p i q c", i=2, c=HC)
        HF = sb("HF", [P, NB, PC], F32)
        MV = sb("MV", [P, NB, 2], F32)
        ST = sb("ST", [P, 4, 6], F32)
        RS = sb("RS", [P, NB], F32)
        NM = sb("NM", [P, NB], F32)
        HB = sb("HB", [P, 2, 4, D], F32)
        HT = sb("HT", [P, 2, 512], F32)
        SG = sb("SG", [P, NB, HEADS], F32)
        SR = sb("SR", [P, 2, P], F32)
        WC = sb("WC", [P, PC], F32)
        WF = sb("WF", [P, HEADS, HD], F32)
        WT = sb("WT", [P, P], F32)
        ABL = sb("ABL", [P, 2 * HEADS], F32)
        ID = sb("ID", [P, P], F32)
        ONES = sb("ONES", [P, P], F32)
        EPSC = sb("EPSC", [P, 1], F32)
        MX = sb("MX", [P, HEADS + 1], F32)
        MH = sb("MH", [P, OCT], F32)
        GM = sb("GM", [P, HEADS + 1], F32)
        NEGT = sb("NEGT", [P, 8], F32)
        EB = sb("EB", [P, 2, NB, HEADS], F32)
        Y = sb("Y", [P, 2, NB, HEADS], F32)
        YS = sb("YS", [P, NB, HEADS], F32)
        RH = sb("RH", [P, 1], F32)
        PT = ps("PT", [P, 2, 512])
        PP = ps("PP", [P, 4, 512])
        PR = ps("PR", [P, 2, P])

        x_in = [sem(f"x_in{u}") for u in range(OCT)]
        w_in, w_mem, v_ps, v_sb = sem("w_in"), sem("w_mem"), sem("v_ps"), sem("v_sb")
        stats, moments, std, norm_ready = sem("stats"), sem("moments"), sem("std"), sem("norm_ready")
        h_ready = sem("h_ready")
        turned = sem("turned")
        projected = sem("projected")
        ht_ready = sem("ht_ready")
        hf_ready = sem("hf_ready")
        s_gathered, srows_ps, sr_ready, sr_out = sem("s_gathered"), sem("srows_ps"), sem("sr_ready"), sem("sr_out")
        maxima, all_max, neg_max, scales = sem("maxima"), sem("all_max"), sem("neg_max"), sem("scales")
        row_args, exps, full, hi_done = sem("row_args"), sem("exps"), sem("full"), sem("hi_done")
        lo_done, mean_ps, largest = sem("lo_done"), sem("mean_ps"), sem("largest")
        x_q = x.rearrange("(u p b) d -> u p b d", u=OCT, b=PLANES)
        block = ctx.enter_context(nc.Block())

        @block.sync
        def _(sp):
            for u in range(OCT):
                sp.dma_start(XQ[:, PLANES * u:PLANES * u + PLANES, :], x_q[u]).then_inc(x_in[u], 16)
            sp.dma_start(ID[:], ident).then_inc(w_in, 16)
            sp.dma_start(WF[:], W.rearrange("h i d -> i h d")).then_inc(w_in, 16)
            sp.dma_start(packing.PW[:], packing.packw).then_inc(packing.weights_in, 16)
            sp.wait_ge(w_mem, 2)
            for s in range(2):
                for h in range(HEADS):
                    sp.dma_start(ABL[HD * h:HD * h + HD, HEADS * s + h:HEADS * s + h + 1],
                                 a[h, HD * s:HD * s + HD, :]).then_inc(w_in, 16)
            sp.wait_ge(sr_ready, 1)
            rows = srow_dram.rearrange("h (half q p) -> half q h p", half=2, p=P)
            for half in range(2):
                sp.dma_start(rows[half], SR[:, half, :]).then_inc(sr_out, 16)
            sp.wait_ge(sr_out, 32)

        @block.tensor
        def _(pe):
            def turn(n, s):
                pe.wait_ge(h_ready, n + 1)
                pe.wait_ge(ht_ready, n + 1)
                for k in range(4):
                    mm = pe.transpose(PT[:, s, k * P:(k + 1) * P], HB[:, s, k, :], ID[:])
                mm.then_inc(turned, 1)

            def project(n, s):
                pe.wait_ge(ht_ready, n + 3)
                pe.wait_ge(hf_ready, n * 2 + 1)
                for k in range(4):
                    mm = pe.matmul(PP[:, 2 * s + k // 2, (k % 2) * PC:(k % 2) * PC + PC],
                                   HT[:, s, k * P:(k + 1) * P], WC[:], start=True, stop=True)
                mm.then_inc(projected, 1)

            pe.sem_inc(turned, 2)
            pe.sem_inc(projected, 2)
            pe.sem_inc(packing.strips_packed, STRIPS)
            pe.wait_ge(w_in, 160)
            pe.transpose(PT[:, 0, 0:P], WF[:].rearrange("p h d -> p (h d)"), ID[:]).then_inc(v_ps, 1)
            pe.wait_ge(v_sb, 1)
            pe.matmul(PT[:, 1, 0:2 * HEADS], WT[:], ABL[:], start=True, stop=True).then_inc(v_ps, 1)
            pe.wait_ge(v_sb, 3)
            pe.wait_ge(packing.weights_in, 16)
            with nc.tensor.Fori(0, 4) as i:
                for pair in range(2):
                    for s in range(2):
                        turn(i * 4 + (2 * pair + s), s)
                    for s in range(2):
                        project(i * 4 + (2 * pair + s), s)
                        for o in range(2):
                            packing.pack(pe, i, 4 * pair + 2 * s + o)
            pe.wait_ge(s_gathered, 1)
            for half in range(2):
                t = pe.transpose(PR[:, half, :], SG[:, 32 * half:32 * half + 32, :].rearrange("p q h -> p (q h)"), ID[:])
            t.then_inc(srows_ps, 1)
            pe.wait_ge(hf_ready, 2 * 16 + 3)
            for qb in range(NB):
                mm = pe.matmul(PT[:, 0, 0:D], ONES[:],
                               HF[:, qb, 0:HEADS * HC].rearrange("p (h c) -> p h c", c=HC)[:, :, 0:HD],
                               start=(qb == 0), stop=(qb == NB - 1))
                if qb % 16 == 15 and qb < NB - 1:
                    for o in range(8):
                        packing.pack(pe, 4 + qb // 16, o)
            mm.then_inc(mean_ps, 1)
            for o in range(8):
                packing.pack(pe, 7, o)

        @block.scalar
        def _(act):
            act.sem_inc(packing.pk_ready, 1)
            act.wait_ge(moments, NB)
            act.wait_ge(w_mem, 4)
            act.activation(RS[:], MV[:, :, 1], ACT.Sqrt, bias=EPSC[:]).then_inc(std, 1)
            act.wait_ge(norm_ready, 2)
            with nc.scalar.Fori(0, 4) as i:
                for v in range(4):
                    act.wait_ge(turned, i * 4 + (v + 1))
                    for k in range(4):
                        qb = i * 16 + 4 * v + k
                        a_ = act.activation(HB[:, v % 2, k, :], XQ[:, ds(qb, 1), :].squeeze(1), ACT.Relu,
                                            bias=NM[:, ds(qb, 1)], scale=RS[:, ds(qb, 1)])
                    a_.then_inc(h_ready, 1)
                packing.keep(act, i, 0, i * 8)
            packing.keep(act, 4, 0, 32)
            act.wait_ge(neg_max, 2)
            for h in range(HEADS):
                t_h = HF[:, :, HEADS * HC + h]
                act.activation(EB[:, 0, :, h], t_h, ACT.Exp, bias=NEGT[:, h:h + 1]).then_inc(exps, 1)
                act.activation(EB[:, 1, :, h], t_h, ACT.Exp, bias=NEGT[:, 4 + h:5 + h], scale=0.2).then_inc(exps, 1)
            act.wait_ge(row_args, 2)
            for c in range(2):
                act.activation(AB[:].rearrange("p q (h c) -> p q h c", c=2)[:, :, :, c], Y[:, c], ACT.Exp) \
                   .then_inc(exps, 1)
            for j in range(2 * HEADS):
                h, c = j // 2, j % 2
                act.wait_ge(full, j + 1)
                act.activation(X[:, :, 0, h, c * HC:(c + 1) * HC], FULL[:, j % 2], ACT.Copy,
                               scale=1.0 / LSCALE).then_inc(hi_done, 1)
                if j in (2, 4, 6):
                    packing.keep(act, 4 + j // 2, 0, 32 + 4 * j)

        @block.gpsimd
        def _(pool):
            pool.memset(WC[:], 0.0).then_inc(w_mem, 1)
            pool.memset(ABL[:], 0.0).then_inc(w_mem, 1)
            pool.memset(ONES[:], 1.0).then_inc(w_mem, 1)
            pool.memset(EPSC[:], EPS).then_inc(w_mem, 1)
            with nc.gpsimd.Fori(0, 5) as T:
                packing.load_tile(pool, T)
            pool.wait_ge(maxima, 2)
            pool.partition_all_reduce(GM[:], MX[:], P, RMAX).then_inc(all_max, 1)
            with nc.gpsimd.Fori(5, 8) as T:
                packing.load_tile(pool, T)

        @block.vector
        def _(dve):
            dve.sem_inc(ht_ready, 2)
            dve.sem_inc(hf_ready, 3)
            for qb in range(NB + 2):
                if qb < NB:
                    if qb % PLANES == 0:
                        dve.wait_ge(x_in[qb // PLANES], 16)
                    if qb >= 4:
                        dve.wait_ge(moments, qb - 3)
                    dve.bn_stats(ST[:, qb % 4, :], XQ[:, qb, :]).then_inc(stats, 1)
                if qb >= 2:
                    dve.wait_ge(stats, qb - 1)
                    dve.bn_aggr(MV[:, qb - 2, :], ST[:, (qb - 2) % 4, :]).then_inc(moments, 1)
            dve.wait_ge(w_mem, 1)
            dve.wait_ge(v_ps, 1)
            dve.tensor_copy(WT[:], PT[:, 0, 0:P]).then_inc(v_sb, 1)
            dve.tensor_copy(WC[:, 0:HEADS * HC].rearrange("p (h c) -> p h c", c=HC)[:, :, 0:HD], WF[:]) \
               .then_inc(v_sb, 1)
            dve.wait_ge(v_ps, 2)
            dve.tensor_copy(WC[:, HEADS * HC:PC], PT[:, 1, 0:2 * HEADS]).then_inc(v_sb, 1)
            dve.wait_ge(std, 1)
            dve.reciprocal(RS[:], RS[:]).then_inc(norm_ready, 1)
            dve.wait_ge(norm_ready, 1)
            dve.scalar_tensor_tensor(NM[:], MV[:, :, 0], -1.0, RS[:], ALU.mult, ALU.mult).then_inc(norm_ready, 1)

            def turned_features(i):
                for s in range(2):
                    dve.wait_ge(turned, i * 2 + (s + 3))
                    dve.wait_ge(projected, i * 2 + (s + 1))
                    dve.tensor_copy(HT[:, s, :], PT[:, s, :]).then_inc(ht_ready, 1)

            def projections(i):
                for s in range(2):
                    dve.wait_ge(projected, i * 2 + (s + 3))
                    for k in range(2):
                        dve.tensor_copy(HF[:, ds(i * 8 + 4 * s + 2 * k, 2), :],
                                        PP[:, 2 * s + k, 0:2 * PC].rearrange("p (k c) -> p k c", c=PC)) \
                           .then_inc(hf_ready, 1)

            def largest_features(i):
                eight = HF[:, ds(i * 8, 8), 0:HEADS * HC]
                dve.wait_ge(hf_ready, i * 4 + 7)
                dve.tensor_reduce(MH[:, ds(i, 1)], eight, AX.XY, ALU.max, apply_absolute_value=True).then_inc(largest, 1)

            turned_features(0)
            projections(0)
            with nc.vector.Fori(1, 8) as i:
                turned_features(i)
                largest_features(i - 1)
                projections(i)
            largest_features(7)
            dve.wait_ge(hf_ready, 2 * 16 + 3)
            tcol = HF[:, :, HEADS * HC:HEADS * HC + HEADS]
            scol = HF[:, :, PC - HEADS:PC]
            dve.tensor_copy(SG[:], scol).then_inc(s_gathered, 1)
            feats = HF[:, :, 0:HEADS * HC]
            dve.tensor_reduce(MX[:, 0:4], tcol.rearrange("p q h -> p h q"), AX.X, ALU.max).then_inc(maxima, 1)
            dve.wait_ge(largest, OCT)
            dve.tensor_reduce(MX[:, HEADS:HEADS + 1], MH[:], AX.X, ALU.max).then_inc(maxima, 1)
            dve.wait_ge(srows_ps, 1)
            dve.tensor_copy(SR[:], PR[:]).then_inc(sr_ready, 1)
            dve.wait_ge(all_max, 1)
            dve.tensor_scalar(NEGT[:, 0:4], GM[:, 0:4], -1.0, None, ALU.mult).then_inc(neg_max, 1)
            dve.tensor_scalar(NEGT[:, 4:8], GM[:, 0:4], -0.2, None, ALU.mult).then_inc(neg_max, 1)
            dve.tensor_scalar(HMAX[:], GM[:, HEADS:HEADS + 1], TINY, None, ALU.max).then_inc(scales, 1)
            dve.tensor_tensor(YS[:], scol, GM[:, 0:4].unsqueeze(1).broadcast_to([P, NB, HEADS]), ALU.add) \
               .then_inc(scales, 1)
            dve.wait_ge(scales, 1)
            dve.reciprocal(RH[:], HMAX[:]).then_inc(scales, 1)
            dve.wait_ge(scales, 2)
            dve.tensor_scalar(Y[:, 0], YS[:], 0.8, 0.0, ALU.mult, ALU.min).then_inc(row_args, 1)
            dve.tensor_scalar(Y[:, 1], YS[:], -0.8, 0.0, ALU.mult, ALU.min).then_inc(row_args, 1)
            dve.tensor_scalar(TB[:], tcol, BIG, None, ALU.mult).then_inc(scales, 1)
            dve.tensor_scalar(NT[:], tcol, -1.0, None, ALU.mult).then_inc(scales, 1)
            dve.wait_ge(exps, 8)
            dve.wait_ge(scales, 3)
            dve.tensor_scalar(EB[:], EB[:], RH[:], XSCALE * LSCALE, ALU.mult, ALU.mult).then_inc(scales, 1)
            dve.tensor_copy(feats.rearrange("p q (h c) -> p q h c", c=HC)[:, :, :, HD],
                            HMAX[:].unsqueeze(2).broadcast_to([P, NB, HEADS])).then_inc(scales, 1)
            dve.wait_ge(scales, 7)
            for j in range(2 * HEADS + 1):
                if j < 2 * HEADS:
                    h, c = j // 2, j % 2
                    if j >= 2:
                        dve.wait_ge(lo_done, j - 1)
                    dve.tensor_tensor(FULL[:, j % 2], HF[:, :, h * HC:(h + 1) * HC],
                                      EB[:, c, :, h].unsqueeze(2).broadcast_to([P, NB, HC]), ALU.mult) \
                       .then_inc(full, 1)
                if j >= 1:
                    h, c = (j - 1) // 2, (j - 1) % 2
                    dve.wait_ge(hi_done, j)
                    dve.scalar_tensor_tensor(X[:, :, 1, h, c * HC:(c + 1) * HC],
                                             X[:, :, 0, h, c * HC:(c + 1) * HC],
                                             -LSCALE, FULL[:, (j - 1) % 2], ALU.mult, ALU.add).then_inc(lo_done, 1)
            dve.wait_ge(mean_ps, 1)
            dve.tensor_scalar(MEAN[:].rearrange("p (h c) -> p h c", c=HD),
                              PT[:, 0, 0:D].rearrange("p (h c) -> p h c", c=HD), 1.0 / N, None, ALU.mult)


def heads_q(v):
    return v.rearrange("(h u p k) d -> u k p h d", h=HEADS, u=OCT, k=2)


def attention_stage(nc, mem, packing, x, srow_dram, x1_dram):
    X, TB, NT, AB, MEAN, HMAX, PK = (mem[n] for n in ("X", "TB", "NT", "AB", "MEAN", "HMAX", "PK"))
    with ExitStack() as ctx:
        sb = lambda n, s, d: ctx.enter_context(nc.sbuf_tensor(n, s, d))
        sem = lambda n: ctx.enter_context(nc.semaphore(n))
        AU = sb("AU", [P, 2, CHUNK, 4, QW], U16)
        MK = sb("MK", [P, SLOTS, HEADS, 512], F8)
        SN = sb("SN", [P, 2, HEADS, 512], F32)
        EV = sb("EV", [P, 7, BANKW], F32)
        MC = sb("MC", [P, 16, 2, HC], F32)
        AC = sb("AC", [P, 16, HC], F32)
        XG = sb("XG", [P, HEADS, 4, HD], F32)
        TM = sb("TM", [P, 16, HD], F32)
        SM = sb("SM", [P, 2, 16], F32)
        acc = [ctx.enter_context(nc.psum_tensor(f"acc{i}", [P, 512], F32)) for i in range(7)]

        waited = sem("waited")
        ep_waited = sem("ep_waited")
        s_in = [sem("s_in0"), sem("s_in1")]
        unpacked = sem("unpacked")
        gt_act, gt_dve = sem("gt_act"), sem("gt_dve")
        masks_ready = sem("masks_ready")
        masks_free = sem("masks_free")
        acc_done = sem("acc_done")
        ev_dve, ev_act = sem("ev_dve"), sem("ev_act")
        ep = sem("ep")
        xg_in, x1_out = sem("xg_in"), sem("x1_out")
        block = ctx.enter_context(nc.Block())

        x_q, x1_q = heads_q(x), heads_q(x1_dram)

        def epilogue(eng, g, i):
            eng.wait_ge(ep, g * EP + (i + 1))
            hi_lo = lambda out, hi, lo: eng.scalar_tensor_tensor(out, lo, 1.0 / LSCALE, hi, ALU.mult, ALU.add)
            pair = lambda bank, s0, s1: EV[:, bank, s0 * 132:s1 * 132].rearrange("p (s c x) -> p s c x", c=2, x=66)
            xg = XG[:].rearrange("p h k x -> p k h x")
            MCf = MC[:].rearrange("p m c x -> p m (c x)")
            if i == 0:
                eng.wait_ge(ev_act, g * 3 + 6)
                eng.wait_ge(ev_dve, g * 4 + 8)
            elif i == 16:
                eng.wait_ge(xg_in, g * 16 + 16)
            eng.sem_inc(ep_waited, 1)
            if i == 0:
                op = hi_lo(AC[:].rearrange("p (k h) x -> p k (h x)", k=4), EV[:, 0:4, 0:132], EV[:, 0:4, 132:264])
            elif i == 1:
                op = hi_lo(MCf.rearrange("p (k h) x -> p k h x", k=4)[:, :, 0, :], EV[:, 0:4, 264:330], EV[:, 0:4, 330:396])
            elif i == 2:
                op = hi_lo(MCf.rearrange("p (k h) x -> p k h x", k=4)[:, 0:3, 3, :], EV[:, 0:3, 396:462], EV[:, 4:7, 396:462])
            elif i <= 7:
                bank, s0, s1, m = [(4, 0, 2, 1), (4, 2, 3, 5), (5, 0, 1, 6), (5, 1, 3, 9), (6, 0, 3, 13)][i - 3]
                op = hi_lo(MCf[:, m:m + s1 - s0, :], pair(bank, s0, s1)[:, :, 0, :], pair(bank, s0, s1)[:, :, 1, :])
            elif i == 8:
                op = eng.tensor_tensor(MC[:, :, 1, :], AC[:], MC[:, :, 1, :], ALU.subtract)
            elif i == 9:
                ab = AB[:, ds(g * 4, 4), :].rearrange("p k c -> p (k c)")
                m = MC[:].rearrange("p m c x -> p (m c) x")
                op = eng.tensor_tensor(m, m, ab.unsqueeze(2).broadcast_to([P, 32, HC]), ALU.mult)
            elif i == 10:
                op = eng.tensor_tensor(AC[:], MC[:, :, 0, :], MC[:, :, 1, :], ALU.add)
            elif i == 11:
                op = eng.tensor_scalar(SM[:, 0, :], AC[:, :, HD], 0.0, None, ALU.is_equal)
            elif i == 12:
                op = eng.tensor_tensor(SM[:, 1, :], AC[:, :, HD], SM[:, 0, :], ALU.add)
            elif i == 13:
                op = eng.reciprocal(SM[:, 1, :], SM[:, 1, :])
            elif i == 14:
                op = eng.tensor_scalar(SM[:, 1, :], SM[:, 1, :], HMAX[:], None, ALU.mult)
            elif i == 15:
                op = eng.tensor_tensor(TM[:], AC[:, :, 0:HD], SM[:, 1, :].unsqueeze(2).broadcast_to([P, 16, HD]), ALU.mult)
            elif i == 16:
                op = eng.tensor_tensor(xg, xg, TM[:].rearrange("p (k h) x -> p k h x", k=4), ALU.add)
            elif i == 17:
                mean = MEAN[:].unsqueeze(1).broadcast_to([P, 4, D]).rearrange("p k (h x) -> p k h x", h=HEADS)
                empty = SM[:, 0, :].unsqueeze(2).broadcast_to([P, 16, HD]).rearrange("p (k h) x -> p k h x", k=4)
                op = eng.tensor_tensor(TM[:].rearrange("p (k h) x -> p k h x", k=4), mean, empty, ALU.mult)
            elif i == 18:
                op = eng.tensor_tensor(xg, xg, TM[:].rearrange("p (k h) x -> p k h x", k=4), ALU.add)
            op.then_inc(ep, 1)

        @block.sync
        def _(sp):
            def load_s(g, slot):
                for h in range(HEADS):
                    sp.dma_start(SN[:, slot, h, :], srow_dram[h:h + 1, ds(g * 512, 512)].broadcast_to([P, 512])) \
                      .then_inc(s_in[slot], 16)

            def load_s_after(g, slot):
                sp.wait_ge(gt_act, g * NB + NB)
                sp.wait_ge(gt_dve, g * NB + NB)
                load_s(g + 2, slot)

            def load_x(u, kp):
                sp.dma_start(XG[:].rearrange("p h k x -> p h (k x)"), x_q[u, kp]).then_inc(xg_in, 16)

            def store_x1(u, kp):
                sp.wait_ge(ep, u * (2 * EP) + (kp * EP + EP + 1))
                sp.dma_start(x1_q[u, kp], XG[:].rearrange("p h k x -> p h (k x)")).then_inc(x1_out, 16)

            def swap_x(u, kp):
                store_x1(u, kp)
                sp.wait_ge(x1_out, u * 32 + (kp * 16 + 16))
                load_x(*((u, 1) if kp == 0 else (u + 1, 0)))

            load_s(0, 0)
            load_s(1, 1)
            load_x(0, 0)
            with nc.sync.Fori(0, OCT - 1) as u:
                load_s_after(u * 2, 0)
                swap_x(u, 0)
                load_s_after(u * 2 + 1, 1)
                swap_x(u, 1)
            swap_x(OCT - 1, 0)
            store_x1(OCT - 1, 1)
            sp.wait_ge(x1_out, 16 * GROUPS)

        @block.gpsimd
        def _(pool):
            def during(g, tiles):
                for j in range(4 * STRIPS):
                    if j // STRIPS < tiles:
                        packing.load_strip(pool, g * 4 + (9 + j // STRIPS), j % STRIPS)
                    if j in EP_POOL_AT:
                        epilogue(pool, g - 1, EP_POOL_AT[j])

            for T in range(8, 13):
                packing.load_tile(pool, T)
            with nc.gpsimd.Fori(1, PACKED_GROUPS - 1) as g:
                during(g, 4)
            during(PACKED_GROUPS - 1, 3)
            for g in (PACKED_GROUPS, PACKED_GROUPS + 1):
                for i in EP_POOL_AT.values():
                    epilogue(pool, g - 1, i)

        @block.tensor
        def _(pe):
            def group(g, packs):
                for n in range(NB):
                    if packs and n in PACK_AT:
                        m, o = PACK_AT[n]
                        packing.pack(pe, g * 4 + (8 + m), o)
                    pe.wait_ge(masks_ready, g * NB + (n + 1))
                    pe.sem_inc(waited, 1)
                    touched = set()
                    for k in range(4):
                        for h, parts, bank, col in pieces(k):
                            if n == 0 and bank not in touched:
                                if bank < 4:
                                    pe.wait_ge(ev_dve, g * 4 + (bank + 1))
                                else:
                                    pe.wait_ge(ev_act, g * 3 + (bank - 3))
                                pe.sem_inc(waited, 1)
                            lo, hi = parts[0], parts[-1] + 1
                            if h is None:
                                lhs = AU[:, n // CHUNK % 2, n % CHUNK, k, :].bitcast(F8)
                                rhs = X[:, n, :, :, HC:2 * HC]
                            else:
                                lhs = MK[:, n % SLOTS, h, k * P:(k + 1) * P]
                                rhs = X[:, n, lo:hi, h, :]
                            width = 66 * (hi - lo) * (HEADS // 2 if h is None else 1)
                            mm = pe.matmul(acc[bank][:, col:col + width], lhs, rhs,
                                           start=(n == 0 and bank not in touched), stop=(n == NB - 1),
                                           skip_group_check=True)
                            touched.add(bank)
                        if n == NB - 1 and k < 3:
                            mm.then_inc(acc_done, 1)
                    mm.then_inc(masks_free, 1)

            pe.sem_inc(masks_free, SLOTS)
            with nc.tensor.Fori(0, PACKED_GROUPS) as g:
                group(g, True)
            with nc.tensor.Fori(PACKED_GROUPS, GROUPS) as g:
                group(g, False)

        @block.scalar
        def _(act):
            def compare(u, kp, n):
                if n == 0:
                    act.wait_ge(s_in[kp], u * 64 + 64)
                act.wait_ge(masks_free, u * (2 * NB) + (kp * NB + n + 1))
                act.sem_inc(waited, 1)
                for h in range(act_heads(n)):
                    c = act.activation(MK[:, n % SLOTS, h, :], SN[:, kp, h, :], ACT.Relu, bias=TB[:, n, h:h + 1],
                                       scale=BIG, saturate=False)
                c.then_inc(gt_act, 1)

            def start(u, kp):
                for n in range(EARLY + 1):
                    compare(u, kp, n)

            def steps(u, kp, packs):
                for n in range(EARLY + 1, NB):
                    compare(u, kp, n)
                    if packs and n in KEEP_AT:
                        t = 4 * kp + KEEP_AT[n]
                        packing.keep(act, u * 8 + (8 + t), u + 1, 8 * t)

            def copy_acc(u, kp):
                g = u * 2 + kp
                act.wait_ge(ep, g * EP + 1)
                for bank, done in ((4, 2), (5, 3)):
                    act.wait_ge(acc_done, g * 3 + done)
                    act.copy(EV[:, bank, :], acc[bank][:, 0:BANKW]).then_inc(ev_act, 1)
                act.wait_ge(masks_free, g * NB + (NB + SLOTS))
                act.copy(EV[:, 6, :], acc[6][:, 0:BANKW]).then_inc(ev_act, 1)

            act.sem_inc(ev_act, 3)
            start(0, 0)
            with nc.scalar.Fori(0, OCT - 1) as u:
                for kp in range(2):
                    steps(u, kp, True)
                    start(*((u, 1) if kp == 0 else (u + 1, 0)))
                    copy_acc(u, kp)
            for kp in range(2):
                steps(OCT - 1, kp, False)
                if kp == 0:
                    start(OCT - 1, 1)
                copy_acc(OCT - 1, kp)

        @block.vector
        def _(dve):
            def unpack(u, kp, q, r):
                b = 4 * kp + r
                if q > 0 or kp > 0 or not isinstance(u, int):
                    dve.wait_ge(masks_free, u * (2 * NB) + (kp * NB + q * CHUNK - CHUNK + SLOTS))
                dve.tensor_scalar(AU[:, q % 2, :, r, :], PK[:, ds(u, 1), CHUNK * q:CHUNK * q + CHUNK, :].squeeze(1),
                                  abs(6 - b), 0x4040,
                                  ALU.logical_shift_left if b <= 6 else ALU.logical_shift_right,
                                  ALU.bitwise_and).then_inc(unpacked, 1)

            def compare(u, kp, n):
                if n == 0:
                    dve.wait_ge(s_in[kp], u * 64 + 64)
                dve.wait_ge(masks_free, u * (2 * NB) + (kp * NB + n + 1))
                dve.sem_inc(waited, 1)
                for h in range(act_heads(n), HEADS):
                    c = dve.tensor_scalar(MK[:, n % SLOTS, h, :], SN[:, kp, h, :], NT[:, n, h:h + 1], 2.0,
                                          ALU.is_gt, ALU.mult, saturate=False)
                c.then_inc(gt_dve, 1)

            def mask(u, kp, n):
                S = u * (2 * NB) + (kp * NB + n)
                if n % CHUNK == 0:
                    dve.wait_ge(unpacked, u * 64 + (kp * 32 + n // CHUNK * 4 + 4))
                dve.wait_ge(gt_dve, S + 1)
                dve.wait_ge(gt_act, S + 1)
                m = MK[:, n % SLOTS].bitcast(U16)
                edges = AU[:, n // CHUNK % 2, n % CHUNK].rearrange("p r w -> p (r w)")
                dve.tensor_tensor(m, m, edges.unsqueeze(1).broadcast_to([P, HEADS, 4 * QW]), ALU.bitwise_and) \
                   .then_inc(masks_ready, 1)

            def start(u, kp):
                if kp == 0:
                    dve.wait_ge(packing.pk_ready, u * 8 + 9)
                for r in range(4):
                    unpack(u, kp, 0, r)
                compare(u, kp, 0)
                for n in range(EARLY):
                    mask(u, kp, n)
                    compare(u, kp, n + 1)

            def copy_acc(u, kp):
                g = u * 2 + kp
                dve.wait_ge(ep, g * EP + 1)
                for k in range(3):
                    dve.wait_ge(acc_done, g * 3 + (k + 1))
                    dve.tensor_copy(EV[:, k, :], acc[k][:, 0:BANKW]).then_inc(ev_dve, 1)
                dve.wait_ge(masks_free, g * NB + (NB + SLOTS))
                dve.tensor_copy(EV[:, 3, 0:396], acc[3][:, 0:396]).then_inc(ev_dve, 1)

            def step(u, kp, n):
                if n >= EARLY:
                    mask(u, kp, n)
                    if n < NB - 1:
                        compare(u, kp, n + 1)
                if n % CHUNK in (3, 4, 5, 6) and n // CHUNK + 1 < NB // CHUNK:
                    unpack(u, kp, n // CHUNK + 1, n % CHUNK - 3)

            dve.sem_inc(ev_dve, 4)
            dve.sem_inc(ep, 1)
            start(0, 0)
            for n in range(NB):
                step(0, 0, n)
            start(0, 1)
            copy_acc(0, 0)
            with nc.vector.Fori(0, OCT - 1) as u:
                for nu, nkp in ((u, 1), (u + 1, 0)):
                    for n in range(NB):
                        step(nu, nkp, n)
                        if n in EP_DVE_AT:
                            epilogue(dve, u * 2 + (1 - nkp), EP_DVE_AT[n])
                    start(*((nu, 1) if nkp == 0 else (nu + 1, 0)))
                    copy_acc(nu, nkp)
            for n in range(NB):
                step(OCT - 1, 1, n)
                if n in EP_DVE_AT:
                    epilogue(dve, GROUPS - 2, EP_DVE_AT[n])
            copy_acc(OCT - 1, 1)
            for i in range(EP):
                epilogue(dve, GROUPS - 1, i)


def graph_stage(nc, mem, ident, ws, wn, ws1, wn1, x1_dram, out):
    PK = mem["PK"]
    with ExitStack() as ctx:
        sb = lambda n, s, d: ctx.enter_context(nc.sbuf_tensor(n, s, d))
        sem = lambda n: ctx.enter_context(nc.semaphore(n))
        HS = sb("HS", [P, NB, 2, D], F16)
        H0T = sb("H0T", [P, N], F32)
        H1T = sb("H1T", [P, N], F32)
        X1 = H1T[:].rearrange("p (q d) -> p q d", d=D)
        ED = sb("ED", [P, SLOTS, 2, PLANES, QW], U16)
        WR = sb("WR", [P, 4, P], F32)
        WT = sb("WTT", [P, 4, P], F32)
        ID = sb("ID2", [P, P], F32)
        MV = sb("MV2", [P, NB, 2], F32)
        ST = sb("ST2", [P, 4, 6], F32)
        RS = sb("RS2", [P, NB], F32)
        NM = sb("NM2", [P, NB], F32)
        EPSC = sb("EPSC2", [P, 1], F32)
        ZB = sb("ZB", [P, 2, 512], F32)
        HB = sb("HB2", [P, 2, 512], F32)
        GB = (HB[:, 0, :], HB[:, 1, :], ZB[:, 0, :], ZB[:, 1, :])
        NH = sb("NH", [P, 2, 512], F32)
        OT = sb("OT", [P, 2, 512], F32)
        XL = sb("XL", [P, 4, 4, D], F32)
        CM = sb("CM", [P, 16], F32)
        SC = sb("SC", [P, 3], F32)
        acc = [ctx.enter_context(nc.psum_tensor(f"sum{i}", [P, 512], F32)) for i in range(4)]
        bank = [ctx.enter_context(nc.psum_tensor(f"bank{i}", [P, 512], F32)) for i in range(4)]

        waited = sem("waited2")
        x1_in = [sem(f"x1_in{u}") for u in range(OCT)]
        consts_in, eps_set, w_turned, w_ready = (
            sem("consts_in2"), sem("eps_set"), sem("w_turned"), sem("w_ready"))
        stats, moments, std, norm_ready = sem("stats2"), sem("moments2"), sem("std2"), sem("norm_ready2")
        z_ready, h_ready = sem("z_ready"), sem("h_ready2")
        turned, h0t_ready = sem("turned2"), sem("h0t_ready")
        hi_ready, lo_ready = sem("hi_ready"), sem("lo_ready")
        g_ready, g_turned = sem("g_ready"), sem("g_turned")
        ed_ready = sem("ed_ready")
        ed_free = sem("ed_free")
        sums_done = sem("sums_done")
        nh_ready = sem("nh_ready")
        post_done = sem("post_done")
        bank_free = sem("bank_free")
        col_max, scale_ready = sem("col_max"), sem("scale_ready")
        ot_ready, ot_turned = sem("ot_ready"), sem("ot_turned")
        xl_in = [sem(f"xl_in{i}") for i in range(4)]
        xl_out = [sem(f"xl_out{i}") for i in range(4)]
        x1_q = x1_dram.rearrange("(u p b) d -> u p b d", u=OCT, b=PLANES)
        out_u, x1_u = (v.rearrange("(u p c b) d -> u c p b d", u=OCT, c=2, b=4) for v in (out, x1_dram))
        block = ctx.enter_context(nc.Block())

        @block.sync
        def _(sp):
            sp.dma_start(ID[:], ident).then_inc(consts_in, 16)
            for i, w in enumerate((ws, wn, ws1, wn1)):
                sp.dma_start(WR[:, i, :], w).then_inc(consts_in, 16)
            for u in range(OCT):
                sp.dma_start(X1[:, PLANES * u:PLANES * u + PLANES, :], x1_q[u]).then_inc(x1_in[u], 16)

            def load_unit(m):
                sp.dma_start(XL[:, m % 4], x1_u[m // 2, m % 2]).then_inc(xl_in[m % 4], 16)

            for m in range(4):
                load_unit(m)
            for m in range(16):
                sp.wait_ge(bank_free, 20 + m + 1)
                sp.dma_start(out_u[m // 2, m % 2], XL[:, m % 4]).then_inc(xl_out[m % 4], 16)
                if m + 4 < 16:
                    sp.wait_ge(xl_out[m % 4], 16 * (m // 4 + 1))
                    load_unit(m + 4)
            for q in xl_out:
                sp.wait_ge(q, 64)

        @block.tensor
        def _(pe):
            def add_up(R, blocks):
                for n in blocks:
                    pe.wait_ge(ed_ready, R * NB + (n + 1))
                    pe.sem_inc(waited, 1)
                    for part in range(2):
                        for m in range(4):
                            if n == 0 and part == 0:
                                pe.wait_ge(nh_ready, R * 4 + (m + 1))
                                pe.sem_inc(waited, 1)
                            edges = ED[:, n % SLOTS, m // 2, m % 2 * 4:m % 2 * 4 + 4, :].rearrange("p b w -> p (b w)").bitcast(F8)
                            mm = pe.matmul(acc[m][:], HS[:, n, part, :], edges,
                                           start=(n == 0 and part == 0), stop=(n == NB - 1 and part == 1))
                            if n == NB - 1 and part == 1 and m < 3:
                                mm.then_inc(sums_done, 1)
                    mm.then_inc(ed_free, 1)

            def combine(R, m, layer, h):
                pe.wait_ge(nh_ready, R * 4 + (m + 5))
                pe.wait_ge(bank_free, R * 4 + (m + 1))
                pe.matmul(bank[m][:], WT[:, 2 * layer, :], h, start=True, stop=False)
                pe.matmul(bank[m][:], WT[:, 2 * layer + 1, :], NH[:, m % 2, :], start=False, stop=True) \
                  .then_inc(post_done, 1)

            def combine_hidden(R):
                for m in range(4):
                    combine(R, m, 0, H0T[:, ds(R * 2048 + 512 * m, 512)])

            def combine_outputs(R):
                for m in range(5):
                    if m < 4:
                        combine(R, m, 1, H1T[:, ds(R * 2048 + (512 * m - 8192), 512)])
                    if m > 0:
                        pe.wait_ge(ot_ready, R * 4 + (m - 16))
                        for k in range(4):
                            t = pe.transpose(bank[m - 1][:, k * P:(k + 1) * P], OT[:, (m - 1) % 2, k * P:(k + 1) * P], ID[:])
                        t.then_inc(ot_turned, 1)

            def turn_features(q):
                pe.wait_ge(h_ready, q + 1)
                pe.wait_ge(h0t_ready, q + 1)
                for k in range(4):
                    t = pe.transpose(bank[q % 2][:, k * P:(k + 1) * P], HB[:, q % 2, k * P:(k + 1) * P], ID[:])
                t.then_inc(turned, 1)

            def turn_hidden(q):
                pe.wait_ge(g_ready, q + 1)
                if q >= 4:
                    pe.wait_ge(lo_ready, 16 + 2 + q - 3)
                for k in range(4):
                    t = pe.transpose(bank[q % 4][:, k * P:(k + 1) * P], GB[q % 4][:, k * P:(k + 1) * P], ID[:])
                t.then_inc(g_turned, 1)

            pe.sem_inc(ed_free, SLOTS)
            pe.sem_inc(post_done, 2)
            pe.sem_inc(turned, 2)
            pe.wait_ge(consts_in, 80)
            for i in range(4):
                t = pe.transpose(bank[3][:, i * P:(i + 1) * P], WR[:, i, :], ID[:])
            t.then_inc(w_turned, 1)
            turn_features(0)
            for q in range(16):
                if q + 1 < 16:
                    turn_features(q + 1)
                pe.wait_ge(hi_ready, 2 + q + 1)
                pe.wait_ge(lo_ready, 2 + q + 1)
                add_up(0, range(4 * q, 4 * q + 4))
            pe.wait_ge(h0t_ready, 16 + 2)
            pe.wait_ge(w_ready, 1)
            combine_hidden(0)
            with nc.tensor.Fori(1, 4) as R:
                add_up(R, range(NB))
                combine_hidden(R)
            turn_hidden(0)
            turn_hidden(1)
            for q in range(16):
                if q + 2 < 16:
                    turn_hidden(q + 2)
                pe.wait_ge(hi_ready, 18 + q + 1)
                pe.wait_ge(lo_ready, 18 + q + 1)
                add_up(4, range(4 * q, 4 * q + 4))
            combine_outputs(4)
            with nc.tensor.Fori(5, 8) as R:
                add_up(R, range(NB))
                combine_outputs(R)

        @block.scalar
        def _(act):
            act.sem_inc(hi_ready, 2)
            act.wait_ge(eps_set, 1)

            act.sem_inc(nh_ready, 4)

            def deviations_of(u):
                act.wait_ge(moments, PLANES * u + PLANES)
                act.activation(RS[:, PLANES * u:PLANES * u + PLANES], MV[:, PLANES * u:PLANES * u + PLANES, 1],
                               ACT.Sqrt, bias=EPSC[:], scale=HSCALE ** -2).then_inc(std, 1)

            deviations_of(0)

            def features(q):
                act.wait_ge(z_ready, q + 1)
                act.wait_ge(turned, q + 1)
                act.wait_ge(lo_ready, q + 1)
                act.activation(HB[:, q % 2, :], ZB[:, q % 2, :], ACT.Relu).then_inc(h_ready, 1)

            def keep_turned(q):
                act.wait_ge(turned, q + 3)
                act.copy(H0T[:, 512 * q:512 * q + 512], bank[q % 2][:]).then_inc(h0t_ready, 1)

            for q in range(16):
                features(q)
                if q > 0:
                    keep_turned(q - 1)
                act.activation(HS[:, 4 * q:4 * q + 4, 0, :], ZB[:, q % 2, :].rearrange("p (k d) -> p k d", d=D),
                               ACT.Relu).then_inc(hi_ready, 1)
                if q % 2 == 1 and q < 15:
                    deviations_of((q + 1) // 2)
            keep_turned(15)

            def neighbours(R, scale):
                for m in range(4):
                    if m < 3:
                        act.wait_ge(sums_done, R * 3 + (m + 1))
                    else:
                        act.wait_ge(ed_free, R * NB + (NB + SLOTS))
                    act.wait_ge(post_done, R * 4 + (m + 1))
                    act.activation(NH[:, m % 2, :], acc[m][:], ACT.Copy, scale=scale).then_inc(nh_ready, 1)

            with nc.scalar.Fori(0, 4) as R:
                neighbours(R, 0.5)
            for q in range(16):
                act.wait_ge(g_turned, q + 1)
                act.copy(HS[:, 4 * q:4 * q + 4, 0, :], bank[q % 4][:].rearrange("p (k d) -> p k d", d=D)) \
                   .then_inc(hi_ready, 1)
            with nc.scalar.Fori(4, 8) as R:
                neighbours(R, SC[:, 2:3])

        @block.gpsimd
        def _(pool):
            pool.memset(EPSC[:], EPS * HSCALE ** -2).then_inc(eps_set, 1)

        @block.vector
        def _(dve):
            def unpack(R, p, n, slot):
                dve.wait_ge(ed_free, n + (R * NB + 1))
                for b in range(PLANES):
                    op = dve.tensor_scalar(ED[:, slot, :, b, :], PK[:, 2 * p:2 * p + 2, ds(n, 1), :].squeeze(2),
                                           abs(6 - b), 0x4040,
                                           ALU.logical_shift_left if b <= 6 else ALU.logical_shift_right,
                                           ALU.bitwise_and)
                op.then_inc(ed_ready, 1)

            dve.sem_inc(bank_free, 4)
            dve.sem_inc(h0t_ready, 2)
            dve.sem_inc(lo_ready, 2)
            dve.wait_ge(w_turned, 1)
            dve.tensor_copy(WT[:].rearrange("p a b -> p (a b)"), bank[3][:]).then_inc(w_ready, 1)

            def moments_of(u):
                dve.wait_ge(x1_in[u], 16)
                for qb in range(PLANES * u, PLANES * u + PLANES + 2):
                    if qb < PLANES * u + PLANES:
                        if qb >= 4:
                            dve.wait_ge(moments, qb - 3)
                        dve.bn_stats(ST[:, qb % 4, :], X1[:, qb, :]).then_inc(stats, 1)
                    if qb >= PLANES * u + 2:
                        dve.wait_ge(stats, qb - 1)
                        dve.bn_aggr(MV[:, qb - 2, :], ST[:, (qb - 2) % 4, :]).then_inc(moments, 1)

            def scales_of(u):
                o = slice(PLANES * u, PLANES * u + PLANES)
                dve.wait_ge(std, u + 1)
                dve.reciprocal(RS[:, o], RS[:, o]).then_inc(norm_ready, 1)
                dve.wait_ge(norm_ready, 2 * u + 1)
                dve.scalar_tensor_tensor(NM[:, o], MV[:, o, 0], -1.0, RS[:, o], ALU.mult, ALU.mult).then_inc(norm_ready, 1)
                dve.wait_ge(norm_ready, 2 * u + 2)

            def normalise(q):
                dve.wait_ge(hi_ready, q + 1)
                for k in range(4):
                    qb = 4 * q + k
                    op = dve.tensor_scalar(ZB[:, q % 2, k * P:(k + 1) * P], X1[:, qb, :],
                                           RS[:, qb:qb + 1], NM[:, qb:qb + 1], ALU.mult, ALU.add)
                op.then_inc(z_ready, 1)

            def lo_parts(q):
                dve.wait_ge(hi_ready, q + 3)
                dve.tensor_tensor(HS[:, 4 * q:4 * q + 4, 1, :], HB[:, q % 2, :].rearrange("p (k d) -> p k d", d=D),
                                  HS[:, 4 * q:4 * q + 4, 0, :], ALU.subtract).then_inc(lo_ready, 1)

            def unpack_pass(R, first, last):
                with nc.vector.Fori(first, last) as i:
                    for n in range(SLOTS):
                        unpack(R, R % 4, i * SLOTS + n, n)

            def unpack_four(R, q):
                for n in range(SLOTS):
                    unpack(R, R % 4, q * SLOTS + n, n)

            def hidden(R):
                for m in range(5):
                    U = 4 * R + m
                    if m < 4:
                        dve.wait_ge(post_done, U + 3)
                        dve.tensor_scalar(H1T[:, 512 * U:512 * U + 512], bank[m][:], 1.0 / HSCALE, 0.0,
                                          ALU.mult, ALU.max).then_inc(bank_free, 1)
                    if m > 0:
                        dve.wait_ge(bank_free, 4 + U)
                        dve.tensor_reduce(CM[:, U - 1:U], H1T[:, 512 * U - 512:512 * U], AX.X, ALU.max).then_inc(col_max, 1)

            def scaled_hidden(q):
                if q >= 4:
                    dve.wait_ge(g_turned, q - 3)
                dve.tensor_scalar(GB[q % 4], H1T[:, 512 * q:512 * q + 512], SC[:, 1:2], None, ALU.mult) \
                   .then_inc(g_ready, 1)

            def lo_of_hidden(q):
                dve.wait_ge(hi_ready, 18 + q + 1)
                dve.tensor_tensor(HS[:, 4 * q:4 * q + 4, 1, :], bank[q % 4][:].rearrange("p (k d) -> p k d", d=D),
                                  HS[:, 4 * q:4 * q + 4, 0, :], ALU.subtract).then_inc(lo_ready, 1)

            def output(v):
                if v >= 2:
                    dve.wait_ge(ot_turned, v - 1)
                dve.wait_ge(post_done, 16 + v + 3)
                dve.tensor_scalar(OT[:, v % 2, :], bank[v % 4][:], 0.0, None, ALU.max).then_inc(ot_ready, 1)

            def result(v):
                dve.wait_ge(ot_turned, v + 1)
                dve.wait_ge(xl_in[v % 4], 16 * (v // 4 + 1))
                xl = XL[:, v % 4].rearrange("p k d -> p (k d)")
                dve.tensor_tensor(xl, xl, bank[v % 4][:], ALU.add).then_inc(bank_free, 1)

            moments_of(0)
            scales_of(0)
            normalise(0)
            for q in range(16):
                if q + 1 < 16:
                    if q % 2 == 1:
                        scales_of((q + 1) // 2)
                    normalise(q + 1)
                lo_parts(q)
                unpack_four(0, q)
                if q % 2 == 0 and q // 2 + 1 < OCT:
                    moments_of(q // 2 + 1)
            for R in range(4):
                unpack_four(R + 1, 0)
                hidden(R)
                if R < 3:
                    unpack_pass(R + 1, 1, 16)
            dve.wait_ge(col_max, 16)
            dve.tensor_reduce(SC[:, 0:1], CM[:], AX.X, ALU.max).then_inc(scale_ready, 1)
            dve.wait_ge(scale_ready, 1)
            dve.tensor_scalar(SC[:, 0:1], SC[:, 0:1], TINY, None, ALU.max).then_inc(scale_ready, 1)
            dve.wait_ge(scale_ready, 2)
            dve.reciprocal(SC[:, 1:2], SC[:, 0:1]).then_inc(scale_ready, 1)
            dve.wait_ge(scale_ready, 3)
            dve.tensor_scalar(SC[:, 1:2], SC[:, 1:2], H1MAX, None, ALU.mult).then_inc(scale_ready, 1)
            dve.tensor_scalar(SC[:, 2:3], SC[:, 0:1], 0.5 / H1MAX, None, ALU.mult).then_inc(scale_ready, 1)
            dve.wait_ge(scale_ready, 5)
            scaled_hidden(0)
            scaled_hidden(1)
            for q in range(16):
                if q + 2 < 16:
                    scaled_hidden(q + 2)
                lo_of_hidden(q)
                if q > 0:
                    unpack_four(4, q)
            for R in range(4, 8):
                if R < 7:
                    unpack_four(R + 1, 0)
                for m in range(5):
                    v = 4 * (R - 4) + m
                    if m < 4:
                        output(v)
                    if m > 0:
                        result(v - 1)
                if R < 7:
                    unpack_pass(R + 1, 1, 16)


def build(nc, x, adj, W, a, ws0, wn0, ws1, wn1, ident, packw, out):
    srow_dram = nc.dram_tensor("srow", (HEADS, N), F32, kind="Internal").ap()
    x1_dram = nc.dram_tensor("x1", (N, D), F32, kind="Internal").ap()
    with ExitStack() as ctx:
        mem = {"PK": ctx.enter_context(nc.sbuf_tensor("PK", [P, OCT, NB, QW], U16))}
        with ExitStack() as inner:
            for name, shape, dt in (("X", [P, NB, 2, HEADS, 2 * HC], F16), ("TB", [P, NB, HEADS], F32),
                                    ("NT", [P, NB, HEADS], F32), ("AB", [P, NB, 2 * HEADS], F32),
                                    ("MEAN", [P, D], F32), ("HMAX", [P, 1], F32)):
                mem[name] = inner.enter_context(nc.sbuf_tensor(name, shape, dt))
            packing = Packing(nc, inner, adj, packw, mem["PK"])
            input_stage(nc, mem, packing, x, W, a, ident, srow_dram)
            attention_stage(nc, mem, packing, x, srow_dram, x1_dram)
        graph_stage(nc, mem, ident, ws0, wn0, ws1, wn1, x1_dram, out)


_INS = ["x", "adj", "L0_gnn_W", "L0_gnn_a", "L1_gnn_w_self_0", "L1_gnn_w_neigh_0", "L1_gnn_w_self_1",
        "L1_gnn_w_neigh_1"]


def kernel(**inputs):
    import concourse.bacc as bacc
    import ml_dtypes
    from concourse.bass_utils import run_bass_kernel_spmd

    nc = bacc.Bacc("TRN2", target_bir_lowering=False, num_devices=1)
    r = np.arange(P)
    packw = np.zeros((P, 8), np.float32)
    packw[r, r // 16] = 2.0 ** (r % 8 + 8 * (r // 8 % 2))
    arrays = {name: np.ascontiguousarray(inputs[name]) for name in _INS}
    arrays["identity"] = np.eye(P, dtype=np.float32)
    arrays["pack_weights"] = packw.astype(ml_dtypes.bfloat16)
    arrays = {f"in_{n}": v for n, v in arrays.items()}
    args = [nc.dram_tensor(n, v.shape, mybir.dt.from_np(v.dtype), kind="ExternalInput").ap()
            for n, v in arrays.items()]
    out = nc.dram_tensor("out_0", (N, D), F32, kind="ExternalOutput").ap()
    build(nc, *args, out)
    r = run_bass_kernel_spmd(nc, [arrays], core_ids=[0])
    return r.results[0]["out_0"]
```
